# Optimizing a Trainium2 kernel written in Bass

```python
import numpy as np
import jax
import jax.numpy as jnp

def _softmax(x, axis=-1):
    return jax.nn.softmax(x, axis=axis)

def _gelu(x):
    return jax.nn.gelu(x, approximate=True)

def _silu(x):
    return jax.nn.silu(x)

def _sigmoid(x):
    return jax.nn.sigmoid(x)

def _layernorm(x, axis=-1, eps=1e-05):
    m = jnp.mean(x, axis=axis, keepdims=True)
    v = jnp.var(x, axis=axis, keepdims=True)
    return (x - m) / jnp.sqrt(v + eps)

def _scatter_add(tgt, idx, src, axis=0):
    return tgt.at[idx].add(src)

def _segment_sum(src, seg, n):
    return jax.ops.segment_sum(src, seg, n)
kernel_name = 'mk_adaln_d1_jaxref_r8_c929d4'

def setup_inputs(seed: int=0):
    np.random.seed(seed)
    _w = jnp.asarray

    def _L0_attn_setup():
        import jax, jax.numpy as jnp
        import numpy as np
        import math
        EMBED = 128
        HEADS = 16
        HEAD_DIM = EMBED // HEADS
        HIDDEN = 512
        NUM_BUCKETS = 32
        MAX_DISTANCE = 128
        LN_EPS = 1e-06
        KQ_EPS = 1e-06

        def _rms_norm(xs, weight):
            xf = xs.astype(jnp.float32)
            var = jnp.mean(jnp.square(xf), axis=-1, keepdims=True)
            ys = xs * jax.lax.rsqrt(var + LN_EPS) * weight
            return ys.astype(xs.dtype)

        def _normalize_kq(kq):
            ss = jnp.sum(jnp.square(kq), axis=-1, keepdims=True)
            return kq * jax.lax.rsqrt(ss + KQ_EPS)

        def _rel_position_bucket(rp):
            rp = -jnp.minimum(rp, 0)
            max_exact = NUM_BUCKETS // 2
            is_small = rp < max_exact
            safe = jnp.maximum(rp, 1).astype(jnp.float32)
            large = max_exact + (jnp.log(safe / max_exact) / math.log(MAX_DISTANCE / max_exact) * (NUM_BUCKETS - max_exact)).astype(jnp.int32)
            large = jnp.minimum(large, NUM_BUCKETS - 1)
            return jnp.where(is_small, rp, large)
        key = jax.random.key(seed)
        ks = jax.random.split(key, 8)
        B, S = (2, 256)
        w = 0.02
        return {'x': jax.random.normal(ks[0], (B, S, EMBED), dtype=jnp.float32), 'ln1_w': jnp.ones((EMBED,), jnp.float32), 'Wq': jax.random.normal(ks[1], (EMBED, EMBED), jnp.float32) * w, 'Wk': jax.random.normal(ks[2], (EMBED, EMBED), jnp.float32) * w, 'Wv': jax.random.normal(ks[3], (EMBED, EMBED), jnp.float32) * w, 'rel_bias': jax.random.normal(ks[4], (NUM_BUCKETS, HEADS), jnp.float32) * w, 'scale': jnp.ones((HEADS,), jnp.float32), 'Wo': jax.random.normal(ks[5], (EMBED, EMBED), jnp.float32) * w, 'ln2_w': jnp.ones((EMBED,), jnp.float32), 'W1': jax.random.normal(ks[6], (EMBED, HIDDEN), jnp.float32) * w, 'W2': jax.random.normal(ks[7], (HIDDEN, EMBED), jnp.float32) * w}
    _L0_attn_in = _L0_attn_setup()

    def _L0_ffn_setup():
        import jax, jax.numpy as jnp
        import numpy as np
        E = 32
        K = 4
        H = 128
        I = 96
        ROUTED_SCALING_FACTOR = 1.0
        key = jax.random.key(seed)
        k0, k1, k2, k3, k4, k5 = jax.random.split(key, 6)
        return {'hidden_states': jax.random.normal(k0, (1, 256, H), jnp.float32), 'gate_w': jax.random.normal(k1, (E, H), jnp.float32) * 0.02, 'w1': jax.random.normal(k2, (E, H, I), jnp.float32) * 0.02, 'w3': jax.random.normal(k3, (E, H, I), jnp.float32) * 0.02, 'w2': jax.random.normal(k4, (E, I, H), jnp.float32) * 0.02, 'e_bias': jax.random.normal(k5, (E,), jnp.float32) * 0.02}
    _L0_ffn_in = _L0_ffn_setup()
    _L0_c = _w((lambda *s: np.random.randn(*s).astype(np.float32) * 0.05)(16, 128))
    _L0_wmod = _w((lambda *s: np.random.randn(*s).astype(np.float32) * 0.05)(128, 6 * 128) * 128 ** (-0.5))
    _d = {'L0_attn_x': _L0_attn_in['x'], 'L0_attn_ln1_w': _L0_attn_in['ln1_w'], 'L0_attn_Wq': _L0_attn_in['Wq'], 'L0_attn_Wk': _L0_attn_in['Wk'], 'L0_attn_Wv': _L0_attn_in['Wv'], 'L0_attn_rel_bias': _L0_attn_in['rel_bias'], 'L0_attn_scale': _L0_attn_in['scale'], 'L0_attn_Wo': _L0_attn_in['Wo'], 'L0_attn_ln2_w': _L0_attn_in['ln2_w'], 'L0_attn_W1': _L0_attn_in['W1'], 'L0_attn_W2': _L0_attn_in['W2'], 'L0_ffn_gate_w': _L0_ffn_in['gate_w'], 'L0_ffn_w1': _L0_ffn_in['w1'], 'L0_ffn_w3': _L0_ffn_in['w3'], 'L0_ffn_w2': _L0_ffn_in['w2'], 'L0_ffn_e_bias': _L0_ffn_in['e_bias'], 'L0_c': _L0_c, 'L0_wmod': _L0_wmod}
    _x0 = _d['L0_attn_x']
    _d['L0_attn_x'] = jax.random.normal(jax.random.fold_in(jax.random.key(seed), 1), (16, 256, 128), dtype=_x0.dtype)
    del _x0
    return _d

def reference(L0_attn_x, L0_attn_ln1_w, L0_attn_Wq, L0_attn_Wk, L0_attn_Wv, L0_attn_rel_bias, L0_attn_scale, L0_attn_Wo, L0_attn_ln2_w, L0_attn_W1, L0_attn_W2, L0_ffn_gate_w, L0_ffn_w1, L0_ffn_w3, L0_ffn_w2, L0_ffn_e_bias, L0_c, L0_wmod):

    def _L0_attn_ref(x, ln1_w, Wq, Wk, Wv, rel_bias, scale, Wo, ln2_w, W1, W2):
        import jax, jax.numpy as jnp
        import numpy as np
        import math
        EMBED = 128
        HEADS = 16
        HEAD_DIM = EMBED // HEADS
        HIDDEN = 512
        NUM_BUCKETS = 32
        MAX_DISTANCE = 128
        LN_EPS = 1e-06
        KQ_EPS = 1e-06

        def _rms_norm(xs, weight):
            xf = xs.astype(jnp.float32)
            var = jnp.mean(jnp.square(xf), axis=-1, keepdims=True)
            ys = xs * jax.lax.rsqrt(var + LN_EPS) * weight
            return ys.astype(xs.dtype)

        def _normalize_kq(kq):
            ss = jnp.sum(jnp.square(kq), axis=-1, keepdims=True)
            return kq * jax.lax.rsqrt(ss + KQ_EPS)

        def _rel_position_bucket(rp):
            rp = -jnp.minimum(rp, 0)
            max_exact = NUM_BUCKETS // 2
            is_small = rp < max_exact
            safe = jnp.maximum(rp, 1).astype(jnp.float32)
            large = max_exact + (jnp.log(safe / max_exact) / math.log(MAX_DISTANCE / max_exact) * (NUM_BUCKETS - max_exact)).astype(jnp.int32)
            large = jnp.minimum(large, NUM_BUCKETS - 1)
            return jnp.where(is_small, rp, large)
        B, S, E = x.shape
        xn = _rms_norm(x, ln1_w)
        q = (xn @ Wq).reshape(B, S, HEADS, HEAD_DIM)
        k = (xn @ Wk).reshape(B, S, HEADS, HEAD_DIM)
        v = (xn @ Wv).reshape(B, S, HEADS, HEAD_DIM)
        q = _normalize_kq(q)
        k = _normalize_kq(k)
        pos = jnp.arange(S, dtype=jnp.int32)
        bucket = _rel_position_bucket(pos[None, :] - pos[:, None])
        bias = rel_bias[bucket]
        bias = jnp.transpose(bias, (2, 0, 1))[None]
        attn = jnp.einsum('bqhd,bkhd->bhqk', q, k) + bias
        attn = attn * scale[None, :, None, None]
        causal = pos[None, :] - pos[:, None] < 0
        attn = jnp.where(causal[None, None], attn, -1000000.0)
        attn = jax.nn.softmax(attn, axis=-1)
        y = jnp.einsum('bhqk,bkhd->bqhd', attn, v).reshape(B, S, E)
        y = y @ Wo + x
        z = _rms_norm(y, ln2_w)
        z = jax.nn.relu(z @ W1) @ W2
        return z + y

    def _L0_ffn_ref(hidden_states, gate_w, w1, w3, w2, e_bias):
        import jax, jax.numpy as jnp
        import numpy as np
        E = 32
        K = 4
        H = 128
        I = 96
        ROUTED_SCALING_FACTOR = 1.0
        orig_shape = hidden_states.shape
        x = hidden_states.reshape(-1, orig_shape[-1])
        T = x.shape[0]
        router_logits = x @ gate_w.T
        scores = jax.nn.sigmoid(router_logits.astype(jnp.float32))
        _, topk_ids = jax.lax.top_k(scores + e_bias[None, :], K)
        topk_w = jnp.take_along_axis(scores, topk_ids, axis=1)
        topk_w = topk_w / jnp.sum(topk_w, axis=1, keepdims=True)
        combine = jnp.zeros((T, E), jnp.float32).at[jnp.arange(T)[:, None], topk_ids].add(topk_w)
        g = jnp.einsum('th,ehi->tei', x, w1)
        u = jnp.einsum('th,ehi->tei', x, w3)
        a = jax.nn.silu(g) * u * combine[:, :, None].astype(x.dtype)
        out = jnp.einsum('tei,eih->th', a, w2)
        out = out * ROUTED_SCALING_FACTOR
        return out.reshape(orig_shape)
    x = L0_attn_x
    mod = (_silu(L0_c) @ L0_wmod).reshape(L0_c.shape[0], 6, 1, -1)
    sa, ca, ga, sb, cb, gb = (mod[:, 0], mod[:, 1], mod[:, 2], mod[:, 3], mod[:, 4], mod[:, 5])
    ga = (2 * (ga >= 0) - 1) * jnp.maximum(jnp.abs(ga), 0.25)
    gb = (2 * (gb >= 0) - 1) * jnp.maximum(jnp.abs(gb), 0.25)
    h = _layernorm(x, axis=-1) * (1 + ca) + sa
    x = x + ga * _L0_attn_ref(h, L0_attn_ln1_w, L0_attn_Wq, L0_attn_Wk, L0_attn_Wv, L0_attn_rel_bias, L0_attn_scale, L0_attn_Wo, L0_attn_ln2_w, L0_attn_W1, L0_attn_W2)
    h = _layernorm(x, axis=-1) * (1 + cb) + sb
    x = x + gb * _L0_ffn_ref(h, L0_ffn_gate_w, L0_ffn_w1, L0_ffn_w3, L0_ffn_w2, L0_ffn_e_bias)
    return x

_drawn_inputs = setup_inputs


def setup_inputs(seed=0):
    import zlib

    import numpy as np

    out = dict(_drawn_inputs(seed))
    spreads = {'L0_attn_ln1_w': (1.0, 0.6), 'L0_attn_scale': (1.0, 0.6), 'L0_attn_ln2_w': (1.0, 0.6)}
    factors = {'L0_attn_Wq': 8.0,
     'L0_attn_Wk': 8.0,
     'L0_attn_Wv': 8.0,
     'L0_attn_rel_bias': 8.0,
     'L0_attn_Wo': 8.0,
     'L0_attn_W1': 3.719,
     'L0_attn_W2': 3.129,
     'L0_ffn_gate_w': 8.0,
     'L0_ffn_w1': 8.0,
     'L0_ffn_w3': 8.0,
     'L0_ffn_w2': 8.0,
     'L0_ffn_e_bias': 8.0}
    for name, (base, spread) in spreads.items():
        noise = np.random.default_rng([zlib.crc32(name.encode()), seed]).standard_normal(out[name].shape)
        drawn = base * np.exp(spread * noise) if base else spread * noise
        out[name] = jnp.asarray(drawn.astype(out[name].dtype))
    for name, factor in factors.items():
        out[name] = (out[name] * factor).astype(out[name].dtype)
    return out
```

```python
from contextlib import ExitStack

import numpy as np
import concourse.bass as bass
from concourse import mybir

ALU = mybir.AluOpType
ACT = mybir.ActivationFunctionType
F32 = mybir.dt.float32
BF16 = mybir.dt.bfloat16
I32 = mybir.dt.int32
U32 = mybir.dt.uint32
AX_X = mybir.AxisListType.X
RMAX = bass.bass_isa.ReduceOp.max

P = 128
NB, SEQ, D = 16, 256, 128
TPB = SEQ // P
NT = NB * TPB
H, HD = 16, 8
HID = 512
NBUCKET, MAXDIST = 32, 128
NE, TOPK, INNER = 32, 4, 96
LN_EPS, RMS_EPS, KQ_EPS = 1e-5, 1e-6, 1e-6
MASKED = -1e30
SAFE = 80.0
RL = 3 * P
UNITS = H // 2
HW = SEQ + P
UW = 2 * HW
SLOT = 64
REGION = NB * SEQ + P
DUMMY = NE * REGION
XTILES = NT * TOPK + NE
XG = 4
XSTEPS = XTILES // XG
S_A, S_B = 0, 2
PRE, CTX = 4, 6


def bucket_one_hot():
    out = np.zeros((NBUCKET, RL), np.float32)
    exact = NBUCKET // 2
    for d in range(1, SEQ):
        if d < exact:
            n = d
        else:
            big = np.log(np.float32(d) / np.float32(exact)) / np.float32(np.log(MAXDIST / exact))
            n = min(exact + int(np.float32(big * np.float32(NBUCKET - exact))), NBUCKET - 1)
        out[n, d + P - 1] = 1.0
    return out


def build(nc, x, ln1_w, Wq, Wk, Wv, rel_bias, scale, Wo, ln2_w, W1, W2, gate_w, w1, w3, w2, e_bias, c, wmod,
          onehot, out):
    ctx = ExitStack()
    with ctx:
        def sb(name, shape, dt=F32):
            return ctx.enter_context(nc.sbuf_tensor(name, shape, dt))

        def sem(name):
            return ctx.enter_context(nc.semaphore(name))

        def dram(name, shape):
            return nc.dram_tensor(name, shape, F32, kind="Internal").ap()

        mod_rows = dram("mod_rows", (NB, 4 * D))
        dist_row = dram("dist_row", (H, RL))
        dist_rep = dram("dist_rep", (H, P, RL))
        xs = dram("xs", (DUMMY + P, D))
        ys = dram("ys", (XTILES * P, D))

        ident = sb("ident", [P, P])
        identb = sb("identb", [P, P], BF16)
        tri = sb("tri", [P, P], BF16)
        onesb = sb("onesb", [P, P], BF16)
        ones = sb("ones", [P, 1])
        iota_e = sb("iota_e", [P, NE])
        tile_no = sb("tile_no", [P, 2])
        wqkv = sb("wqkv", [P, 3 * D])
        wo = sb("wo", [P, D])
        w1s = sb("w1s", [P, HID])
        w2s = sb("w2s", [P, HID // P, D])
        ln1 = sb("ln1", [P, 1])
        ln2 = sb("ln2", [P, 1])
        gate = sb("gate", [NE, D])
        gateT = sb("gateT", [P, NE])
        ebias = sb("ebias", [P, NE])
        srow = sb("srow", [P, H])
        scol = sb("scol", [H, 1])
        qscale = sb("qscale", [P, TPB, H])
        csb = sb("csb", [NB, D])
        cth = sb("cth", [NB, D])
        scT = sb("scT", [P, NB])
        modT = sb("modT", [P, 2 * NB])
        relb = sb("relb", [NBUCKET, H])
        flagf = sb("flagf", [P, 4])
        flagi = sb("flagi", [1, 4], I32)
        modb = sb("modb", [P, NB, 4, D])
        X = sb("X", [P, NT, D])
        Y = sb("Y", [P, NT, D])
        BIAS = sb("BIAS", [P, UNITS, UW])
        w13 = BIAS[:, :, :].rearrange("p u w -> p (u w)")
        w2e = sb("w2e", [INNER, NE, D])
        stats = sb("stats", [P, NT, 6])
        mean = sb("mean", [P, NT])
        var = sb("var", [P, NT])
        rstd = sb("rstd", [P, NT])
        st1 = sb("st1", [P, NT])
        st2 = sb("st2", [P, NT])
        XH = sb("XH", [P, TPB, D])
        hT = [sb(f"hT{i}", [P, SEQ]) for i in range(2)]
        hR = [sb(f"hR{i}", [P, SEQ]) for i in range(2)]
        hsq = sb("hsq", [P, SEQ])
        QKN = sb("QKN", [P, 2 * TPB * P])
        QKR = sb("QKR", [P, 2 * TPB * P])
        sq = QKR
        part = [sb(f"part{i}", [P, 2, TPB * H, HD], BF16) for i in range(3)]
        SLOTS = sb("SLOTS", [P, 2, TPB * H, SLOT], BF16)
        QKT = [sb(f"QKT{i}", [P, 2, UNITS, SEQ], BF16) for i in range(2)]
        V = [sb(f"V{i}", [P, TPB, H, 32]) for i in range(2)]
        NARG = 2 * TPB * H + TPB
        arg = sb("arg", [P, NARG])
        rs = sb("rs", [P, NARG])
        nt1 = sb("nt1", [P, NARG])
        nt2 = sb("nt2", [P, NARG])
        em = sb("em", [P, TPB])
        L = [sb(f"L{i}", [P, UW]) for i in range(2)]
        LM = sb("LM", [P, UW])
        PR = [sb(f"PR{i}", [P, UW]) for i in range(4)]
        YT = sb("YT", [P, H // 4, SEQ])
        rden = sb("rden", [P, TPB, H])
        YN = sb("YN", [P, TPB, D])
        YNT = sb("YNT", [P, SEQ])
        mT = [YT[:, 2 * i, :] for i in range(2)]
        YS = [YT[:, 2 * i + 1, :].rearrange("p (t d) -> p t d", t=TPB) for i in range(2)]
        hid = [sb(f"hid{i}", [P, HID // P, SEQ]) for i in range(2)]
        zt = XH
        hid_flat = [hid[i][:, :, :].rearrange("p c t -> p (c t)") for i in range(2)]
        mrow = hid_flat[1][0:NB, 0:4 * D].rearrange("b (m d) -> b m d", m=4)
        mtmp = hid_flat[1][0:NB, 4 * D:6 * D].rearrange("b (m d) -> b m d", m=2)
        oneh = hid_flat[0][0:NBUCKET, 0:RL]
        drow = hid_flat[0][0:H, RL:2 * RL]
        H2 = [hid[i][:, 0, :].rearrange("p (t d) -> p t d", t=TPB) for i in range(2)]
        H2T = [hid[i][:, 1, :] for i in range(2)]
        th = sb("th", [P, TPB, NE])
        score = sb("score", [P, TPB, NE])
        sel = sb("sel", [P, TPB, NE])
        top = sb("top", [P, TPB, 8])
        topi = sb("topi", [P, TPB, 8], U32)
        OH = sb("OH", [P, TPB, TOPK, NE])
        OHT = sb("OHT", [P, TPB, TOPK, NE])
        maskb = sb("maskb", [P, TPB, NE], BF16)
        seen = sb("seen", [P, NE], BF16)
        rank = sb("rank", [P, TPB, NE])
        rk = sb("rk", [P, TPB * TOPK])
        wsum = sb("wsum", [P, TPB])
        posi = [sb(f"posi{i}", [P, TPB * TOPK], I32) for i in range(2)]
        IDX = sb("IDX", [P, NT * TOPK])
        RK = sb("RK", [P, NT * TOPK])
        WT = sb("WT", [P, NT * TOPK])
        cnt = sb("cnt", [P, NE])
        cnti = sb("cnti", [P, NE], I32)
        ntile = sb("ntile", [P, NE])
        tend = sb("tend", [P, NE])
        tstart = sb("tstart", [P, NE])
        onesf = sb("onesf", [P, NE])
        ge = sb("ge", [P, 2, NE])
        ge2 = sb("ge2", [P, 2, NE])
        tv = sb("tv", [P, 4])
        treg = sb("treg", [1, 4, P], I32)
        rowi = sb("rowi", [1, NE], I32)
        POS = sb("POS", [P, NT * TOPK], I32)
        BIG = V[0][:, :, :, :].rearrange("p t h s -> p (t h s)")
        zeros = hid[0][:, 2, 0:P]
        xg = [PR[i][:, 0:XG * P] for i in range(2)]
        xgT = [PR[2 + i][:, 0:XG * P] for i in range(2)]
        sg = [L[i][:, 0:XG * INNER] for i in range(2)]
        aa = [QKN[:, 0:XG * INNER], QKR[:, 0:XG * INNER]]
        aT = hid[1][:, 0:2, :].rearrange("p a b -> p (a b)")
        yo = [hid[1][:, 2:4, :].rearrange("p a b -> p (a b)"), YT[:, 0:2, :].rearrange("p a b -> p (a b)")]
        gidx = [sb(f"gidx{i}", [P, TOPK], I32) for i in range(2)]
        G = [SLOTS[:, i, :, :].rearrange("p a b -> p (a b)").bitcast(F32)[:, 0:TOPK * D]
             .rearrange("p (k d) -> p k d", k=TOPK) for i in range(2)]
        acc = [sb(f"acc{i}", [P, D]) for i in range(2)]

        PS = ctx.enter_context(nc.psum_tensor("PS", [P, 8, 512], F32))

        names = """ld_c ld_x ld_w ld_b ld_e pool_c pool_s credit
            sc_act sc_dve sc_pe md_pe md_dve wr_mod ld_mod gt_pe gt_dve dr_pe dr_dve wr_dist rep_dist ld_bias bias0
            dve_s ln_ready flag_ready
            xh_ready xt_done hT_ready qkv_done sq_done rs_done v_ready qn_done split_done slots_ready qkt_done
            qkt_act qkt_dve qk_done l_ready g_max g_in g_dve exp_done pv_done yt_ready o2_done o3_done o4_done
            ynt_ready o5_done y_ready
            c_s ys_staged m_t m_tev m_hid relu_act relu_dve m_z z_done x_done
            r_s h2_ready r_t r_tev r_lg r_th r_mask r_rank r_evac pos_ready
            d_s cnt_pe zero_ready zero_done x_meta x_rows0 x_rows1 sc_done tv_pe tv_ready rows_ready t_ready w_free
            xt_pe xt_ev gu_pe sg_act a_dve at_pe at_act y_pe y_ev yst0 yst1 pos_all settled hr_ready
            idx_in gsem0 gsem1 acc_s acc_ready g_free ost0 ost1 e_s scat0 scat1 pool_g""".split()
        s = {n: sem(n) for n in names}
        block = ctx.enter_context(nc.Block())

        def bank(b, n=512, m=0):
            return PS[:, b, m:m + n]

        def settle(eng):
            eng.sem_inc(s["settled"], 1)

        class Steps:
            def __init__(self, eng, name, start=0):
                self.eng, self.sem, self.n, self.at = eng, s[name], start, 0

            def __call__(self, ins):
                ins.then_inc(self.sem, 1)
                self.n += 1
                return ins

            def wait(self):
                self.eng.wait_ge(self.sem, self.at + self.n)

        def rsqrt(dve, step, y, a, t1, t2):
            step(dve.tensor_scalar(t1.bitcast(I32), a.bitcast(I32), 1, None, ALU.logical_shift_right))
            step.wait()
            step(dve.tensor_scalar(y.bitcast(I32), t1.bitcast(I32), -1.0, float(0x5f3759df), ALU.mult, ALU.add))
            for _ in range(4):
                step.wait()
                step(dve.tensor_tensor(t1, y, y, ALU.mult))
                step.wait()
                step(dve.scalar_tensor_tensor(t2, t1, -0.5, a, ALU.mult, ALU.mult))
                step.wait()
                last = step(dve.scalar_tensor_tensor(y, t2, 1.5, y, ALU.add, ALU.mult))
            return last

        def mean_var(dve, step):
            step.wait()
            step(dve.tensor_tensor(st1[:, :], stats[:, :, 1], stats[:, :, 4], ALU.add))
            step(dve.tensor_tensor(st2[:, :], stats[:, :, 1], stats[:, :, 4], ALU.subtract))
            step(dve.tensor_tensor(rstd[:, :], stats[:, :, 2], stats[:, :, 5], ALU.add))
            step.wait()
            step(dve.tensor_scalar(mean[:, :], st1[:, :], 0.5, None, ALU.mult))
            step(dve.scalar_tensor_tensor(st2[:, :], st2[:, :], 0.25, st2[:, :], ALU.mult, ALU.mult))
            step.wait()
            step(dve.scalar_tensor_tensor(var[:, :], rstd[:, :], 1.0 / D, st2[:, :], ALU.mult, ALU.add))

        def row_stats(dve, step, src):
            with dve.Fori(0, NT) as n:
                dve.bn_stats(stats[:, bass.ds(n, 1), :].rearrange("p a s -> p (a s)"),
                             src[:, bass.ds(n, 1), :].rearrange("p a d -> p (a d)")).then_inc(step.sem, 1)
            step.n += NT

        def tok(buf, b, t=0, n=1):
            return buf[:, bass.ds(b * TPB + t, n), :]

        def tok1(buf, b, t):
            return tok(buf, b, t).rearrange("p a d -> p (a d)")

        @block.sync
        def _(sp):
            for dst, src in ((csb[:, :], c), ):
                sp.dma_start(dst, src).then_inc(s["ld_c"], 16)
            sp.dma_start(modb[:, 0:2, :, :].rearrange("p a b d -> p (a b d)")[:, 0:6 * D], wmod).then_inc(s["ld_c"], 16)
            sp.dma_start(relb[:, :], rel_bias).then_inc(s["ld_b"], 16)
            sp.dma_start(oneh[:, :], onehot).then_inc(s["ld_b"], 16)
            sp.dma_start(scol[:, :], scale.rearrange("(h a) -> h a", a=1)).then_inc(s["ld_b"], 16)
            sp.dma_start(srow[:, :], scale.rearrange("(a h) -> a h", a=1).to_broadcast([P, H])).then_inc(s["ld_b"], 16)
            xv = x.rearrange("b (t p) d -> p (b t) d", p=P)
            for i in range(4):
                sp.dma_start(X[:, i * 8:(i + 1) * 8, :], xv[:, i * 8:(i + 1) * 8, :]).then_inc(s["ld_x"], 16)
            for dst, src in ((wqkv[:, 0:D], Wq), (wqkv[:, D:2 * D], Wk), (wqkv[:, 2 * D:], Wv), (wo[:, :], Wo),
                             (w1s[:, :], W1), (w2s[:, :, :], W2.rearrange("(c p) d -> p c d", p=P)),
                             (ln1[:, :], ln1_w.rearrange("(p a) -> p a", a=1)),
                             (ln2[:, :], ln2_w.rearrange("(p a) -> p a", a=1)), (gate[:, :], gate_w),
                             (ebias[:, :], e_bias.rearrange("(a e) -> a e", a=1).to_broadcast([P, NE])),
                             (w2e[:, :, :], w2.rearrange("e i d -> i e d"))):
                sp.dma_start(dst, src).then_inc(s["ld_w"], 16)
            sp.wait_ge(s["dr_dve"], 2)
            sp.dma_start(dist_row, drow[:, :]).then_inc(s["wr_dist"], 16)
            sp.wait_ge(s["wr_dist"], 16)
            sp.dma_start(dist_rep, dist_row.rearrange("h (a l) -> h a l", a=1).to_broadcast([H, P, RL])).then_inc(s["rep_dist"], 16)
            sp.wait_ge(s["rep_dist"], 16)
            for h in range(H):
                for n, w in ((0, SEQ), (1, P)):
                    src = bass.AP(dist_rep.tensor, h * P * RL + P - 1, [[RL - 1, P], [1, w]])
                    at = (h % 2) * HW + (SEQ if n else 0)
                    sp.dma_start(BIAS[:, h // 2, at:at + w], src).then_inc(s["ld_bias"], 16)
            sp.wait_ge(s["md_dve"], 2)
            sp.dma_start(mod_rows, mrow[:, :, :].rearrange("b m d -> b (m d)")).then_inc(s["wr_mod"], 16)
            sp.wait_ge(s["wr_mod"], 16)
            sp.dma_start(modb[:, :, :, :].rearrange("p b m d -> p (b m d)"),
                         mod_rows.rearrange("b m -> (b m)").rearrange("(a m) -> a m", a=1).to_broadcast([P, NB * 4 * D])
                         ).then_inc(s["ld_mod"], 16)
            sp.wait_ge(s["l_ready"], NB * UNITS + 2)
            w13v = w13.rearrange("p (e g i) -> p e g i", e=NE, g=2)
            sp.dma_start(w13v[:, :, 0, :], w1.rearrange("e d i -> d e i")).then_inc(s["ld_e"], 16)
            sp.dma_start(w13v[:, :, 1, :], w3.rearrange("e d i -> d e i")).then_inc(s["ld_e"], 16)
            sp.wait_ge(s["zero_ready"], 1)
            sp.dma_start(xs[DUMMY:DUMMY + P, :], zeros).then_inc(s["zero_done"], 16)
            sp.wait_ge(s["rows_ready"], 1)
            with sp.Fori(0, NE) as e:
                row = sp.value_load(rowi[0:1, bass.ds(e, 1)], min_val=0, max_val=DUMMY - P)
                sp.dma_start(xs[bass.ds(row, P), :], zeros).then_inc(s["zero_done"], 16)
            sp.wait_ge(s["zero_done"], 16 * (NE + 1))
            sp.wait_ge(s["scat0"], 16 * NT * TOPK // 2)
            sp.wait_ge(s["scat1"], 16 * NT * TOPK // 2)
            sp.wait_ge(s["t_ready"], 1)

            def load_rows(i, par):
                for j in range(XG):
                    row = sp.value_load(treg[0:1, 2:4, :].rearrange("p a b -> p (a b)")[:, bass.ds(i * XG + j, 1)],
                                        min_val=0, max_val=DUMMY)
                    sp.dma_start(xg[par][:, j * P:(j + 1) * P], xs[bass.ds(row, P), :]).then_inc(s[f"x_rows{par}"], 16)

            def store_rows(i, par):
                sp.wait_ge(s["y_ev"], i + 1 + 1)
                sp.dma_start(ys[bass.ds(i * XG * P, XG * P), :].rearrange("(j p) d -> p j d", p=P),
                             yo[par].rearrange("p (j d) -> p j d", j=XG)).then_inc(s[f"yst{par}"], 16)
            load_rows(0, 0)
            load_rows(1, 1)
            with sp.Fori(0, (XSTEPS - 2) // 2) as two:
                i = two * 2
                for par in range(2):
                    sp.wait_ge(s["xt_pe"], i + par + 1)
                    load_rows(i + par + 2, par)
                    store_rows(i + par, par)
            for par in range(2):
                store_rows(XSTEPS - 2 + par, par)
            outv = out.rearrange("b (t p) d -> p (b t) d", p=P)
            with sp.Fori(0, NT // 2) as two:
                n = two * 2
                for par in range(2):
                    sp.wait_ge(s["acc_ready"], n + par + 1)
                    sp.dma_start(outv[:, bass.ds(n + par, 1), :].rearrange("p a d -> p (a d)"),
                                 acc[par][:, :]).then_inc(s[f"ost{par}"], 16)
            for par in range(2):
                sp.wait_ge(s[f"yst{par}"], 16 * XSTEPS // 2)
                sp.wait_ge(s[f"ost{par}"], 16 + 16 * NT // 2)

        @block.gpsimd
        def _(pool):
            st = Steps(pool, "pool_s")
            st(pool.memset(ident[:, :], 0.0))
            st(pool.memset(identb[:, :], 0.0))
            st(pool.memset(tri[:, :], 1.0))
            st.wait()
            for m in (ident, identb):
                pool.affine_select(out=m[:, :], in_=m[:, :], compare_op=ALU.not_equal, fill=1.0, base=0,
                                   pattern=[[-1, P]], channel_multiplier=1)
            pool.affine_select(out=tri[:, :], in_=tri[:, :], compare_op=ALU.is_ge, fill=0.0, base=-1,
                               pattern=[[1, P]], channel_multiplier=-1)
            pool.memset(onesb[:, :], 1.0)
            pool.memset(ones[:, :], 1.0)
            pool.memset(onesf[:, :], 1.0)
            pool.memset(seen[:, :], 0.0)
            pool.iota(iota_e[:, :], [[1, NE]], base=0, channel_multiplier=0, allow_small_or_imprecise_dtypes=True)
            pool.iota(tile_no[:, :], [[P, 2]], base=0, channel_multiplier=1, allow_small_or_imprecise_dtypes=True)
            pool.memset(SLOTS[:, :, :, :], 0.0)
            pool.memset(V[0][:, :, :, :], 0.0)
            st(pool.memset(V[1][:, :, :, :], 0.0))
            st.wait()
            for v in V:
                last = pool.memset(v[:, :, :, HD:HD + 1], 1.0)
            last.then_inc(s["pool_c"], 1)
            pool.wait_ge(s["flag_ready"], 1)
            pool.sem_inc(s["hr_ready"], 2)
            big = pool.value_load(flagi[0:1, 0:1], min_val=0, max_val=1)

            def slots(b):
                pool.wait_ge(s["split_done"], b + 1)
                settle(pool)
                q, k = SLOTS[:, 0, :, :], SLOTS[:, 1, :, :]

                def put(dst, at, n, stride, src, qk):
                    d = dst[:, :, at:at + 8 * (stride * (n - 1) + 1)]
                    if n > 1:
                        d = dst[:, :, at:at + 8 * stride * n].rearrange("p th (n e) -> p th n e", n=n)[:, :, :, 0:8]
                        return pool.tensor_copy(d, src[:, qk, :, :].unsqueeze(2).to_broadcast([P, TPB * H, n, HD]))
                    return pool.tensor_copy(d, src[:, qk, :, :])
                put(q, 0, 2, 3, part[0], 0)
                put(q, 40, 1, 1, part[0], 0)
                put(q, 8, 2, 3, part[1], 0)
                put(q, 16, 1, 1, part[2], 0)
                put(k, 0, 3, 1, part[0], 1)
                put(k, 24, 2, 1, part[1], 1)
                put(k, 40, 1, 1, part[2], 1).then_inc(s["slots_ready"], 1)

            def h_copy(b, par):
                pool.wait_ge(s["o5_done"], b + 1)
                settle(pool)
                pool.wait_ge(s["hT_ready"], b + 1)
                settle(pool)
                pool.tensor_copy(hR[par][:, :], hT[par][:, :]).then_inc(s["hr_ready"], 1)

            def row_max(b):
                with pool.If(big == 1):
                    for u in range(UNITS):
                        pool.wait_ge(s["g_in"], b * UNITS + u + 1)
                        settle(pool)
                        pool.partition_all_reduce(LM[:, :], L[u % 2][:, :], P, RMAX).then_inc(s["g_max"], 1)

            def sequence(b, par, last=False):
                if not last:
                    h_copy(b + 1, 1 - par)
                row_max(b)
                if not last:
                    slots(b + 1)

            h_copy(0, 0)
            slots(0)
            sequence(0, 0)
            with pool.Fori(0, (NB - 2) // 2) as two:
                b = two * 2 + 1
                sequence(b, 1)
                sequence(b + 1, 0)
            sequence(NB - 1, 1, last=True)

            with pool.Fori(0, NB // 2) as two:
                b = two * 2
                for par in range(2):
                    pool.wait_ge(s["pos_ready"], b + par + 1)
                    settle(pool)
                    for t in range(TPB):
                        for k in range(TOPK):
                            pool.indirect_dma_start(
                                out=xs, out_offset=bass.IndirectOffsetOnAxis(
                                    ap=posi[par][:, t * TOPK + k:t * TOPK + k + 1], axis=0),
                                in_=H2[par][:, t, :], in_offset=None).then_inc(s[f"scat{par}"], 16)

            pool.wait_ge(s["pos_all"], 1)
            for par in range(2):
                pool.wait_ge(s[f"yst{par}"], 16 * XSTEPS // 2)
            with pool.Fori(0, NT // 2) as two:
                n = two * 2
                for par in range(2):
                    pool.wait_ge(s["g_free"], n + par + 1)
                    settle(pool)
                    pool.tensor_copy(gidx[par][:, :], POS[:, bass.ds((n + par) * TOPK, TOPK)]).then_inc(s["pool_g"], 1)
                    pool.wait_ge(s["pool_g"], n + par + 1)
                    settle(pool)
                    for k in range(TOPK):
                        pool.indirect_dma_start(out=G[par][:, k, :], out_offset=None, in_=ys,
                                                in_offset=bass.IndirectOffsetOnAxis(ap=gidx[par][:, k:k + 1], axis=0)
                                                ).then_inc(s[f"gsem{par}"], 16)

        @block.scalar
        def _(act):
            act.sem_inc(s["qkt_act"], 2)
            act.sem_inc(s["exp_done"], 2)
            act.sem_inc(s["ynt_ready"], 1)
            act.sem_inc(s["y_ready"], 1)
            act.wait_ge(s["ld_c"], 32)
            act.activation(cth[:, :], csb[:, :], ACT.Tanh, scale=0.5).then_inc(s["sc_act"], 1)

            def make_hT(b, par):
                act.wait_ge(s["xt_done"], b + 1 + 1)
                act.wait_ge(s["hr_ready"], b + 1)
                a, c0 = modT[:, bass.ds(b + NB, 1)], modT[:, bass.ds(b, 1)]
                act.activation(hT[par][:, :], bank(PRE, SEQ), ACT.Identity, bias=c0, scale=a)
                act.activation(hsq[:, :], bank(PRE, SEQ), ACT.Square, bias=c0, scale=a).then_inc(s["hT_ready"], 1)

            def squares(b):
                act.wait_ge(s["qkv_done"], b + 1)
                act.activation(sq[:, :].rearrange("p (q t d) -> p t q d", q=2, t=TPB),
                               PS[:, PRE:PRE + TPB, 0:2 * D].rearrange("p t (q d) -> p t q d", q=2),
                               ACT.Square).then_inc(s["sq_done"], 1)

            def values(b, par):
                act.wait_ge(s["qn_done"], b + 1)
                for t in range(TPB):
                    last = act.activation(V[par][:, t, :, 0:HD],
                                          bank(PRE + t, D, 2 * D).rearrange("p (h d) -> p h d", h=H),
                                          ACT.Identity, scale=rs[:, 2 * TPB * H + t:2 * TPB * H + t + 1])
                last.then_inc(s["v_ready"], 1)

            def qk_half(b, par, qk):
                act.wait_ge(s["qkt_done"], b * 4 + 2 * qk + 1)
                act.activation(QKT[par][:, qk, :, 0:P], bank(PRE).bitcast(BF16).rearrange("p (u t) -> p u t", u=UNITS),
                               ACT.Copy).then_inc(s["qkt_act"], 1)

            def exp(b, u):
                act.wait_ge(s["l_ready"], b * UNITS + u + 1 + 2)
                if u % 2 == 0:
                    act.wait_ge(s["pv_done"], b * 4 + u // 2 + 1)
                act.activation(PR[u % 4][:, :], L[u % 2][:, :], ACT.Exp).then_inc(s["exp_done"], 1)

            def context(b, half):
                act.wait_ge(s["pv_done"], b * 4 + 2 * half + 2 + 2)
                act.activation(YT[:, 2 * half:2 * half + 2, :].rearrange("p g t -> p (g t)"), bank(CTX + half),
                               ACT.Copy).then_inc(s["yt_ready"], 1)

            def yn_T(b):
                act.wait_ge(s["o4_done"], b + 1)
                act.activation(YNT[:, :], bank(CTX, SEQ), ACT.Copy).then_inc(s["ynt_ready"], 1)

            def y_out(b):
                act.wait_ge(s["o5_done"], b + 1 + 2)
                act.activation(tok(Y, b, 0, TPB), bank(CTX + 1, SEQ).rearrange("p (t d) -> p t d", t=TPB),
                               ACT.Copy).then_inc(s["y_ready"], 1)

            def sequence(b, par, first=False, last=False):
                exp(b, 0)
                if not last:
                    make_hT(b + 1, 1 - par)
                exp(b, 1)
                if not last:
                    squares(b + 1)
                if not first:
                    yn_T(b - 1)
                exp(b, 2)
                if not first:
                    y_out(b - 1)
                if not last:
                    values(b + 1, 1 - par)
                exp(b, 3)
                exp(b, 4)
                exp(b, 5)
                context(b, 0)
                exp(b, 6)
                exp(b, 7)
                if not last:
                    qk_half(b + 1, 1 - par, 0)
                context(b, 1)
                if not last:
                    qk_half(b + 1, 1 - par, 1)

            act.wait_ge(s["md_dve"], 1)
            make_hT(0, 0)
            squares(0)
            values(0, 0)
            qk_half(0, 0, 0)
            qk_half(0, 0, 1)
            sequence(0, 0, first=True)
            with act.Fori(0, (NB - 2) // 2) as two:
                b = two * 2 + 1
                sequence(b, 1)
                sequence(b + 1, 0)
            sequence(NB - 1, 1, last=True)
            yn_T(NB - 1)
            y_out(NB - 1)

            with act.Fori(0, NB // 2) as two:
                b = two * 2
                for par in range(2):
                    act.wait_ge(s["m_t"], b + par + 1)
                    act.activation(mT[par], bank(par, SEQ), ACT.Copy).then_inc(s["m_tev"], 1)
                for par in range(2):
                    act.wait_ge(s["m_hid"], b + par + 1)
                    act.activation(hid[par][:, 0:2, :].rearrange("p c t -> p (c t)"), bank(2 + 2 * par),
                                   ACT.Relu).then_inc(s["relu_act"], 1)
            with act.Fori(0, NB // 2) as two:
                b = two * 2
                for par in range(2):
                    act.wait_ge(s["r_t"], b + par + 1)
                    act.activation(H2T[par], bank(4 * par, SEQ), ACT.Copy).then_inc(s["r_tev"], 1)
                    act.wait_ge(s["r_lg"], b + par + 1)
                    act.activation(th[:, :, :].rearrange("p t e -> p (t e)"), bank(4 * par + 1, TPB * NE),
                                   ACT.Tanh, scale=0.5).then_inc(s["r_th"], 1)
            def silu(i, par):
                act.wait_ge(s["gu_pe"], i + 1)
                act.activation(sg[par].rearrange("p (a b i) -> p a b i", a=2, b=2),
                               PS[:, 2 + 2 * par:4 + 2 * par, 0:4 * INNER]
                               .rearrange("p a (b g i) -> p a b g i", b=2, g=2)[:, :, :, 0, :],
                               ACT.Silu).then_inc(s["sg_act"], 1)

            def a_T(i):
                act.wait_ge(s["at_pe"], i + 1)
                act.activation(aT[0:INNER, :], PS[0:INNER, 6, :], ACT.Copy).then_inc(s["at_act"], 1)
            silu(0, 0)
            with act.Fori(0, (XSTEPS - 2) // 2) as two:
                i = two * 2
                for par in range(2):
                    silu(i + par + 1, 1 - par)
                    a_T(i + par)
            silu(XSTEPS - 1, 1)
            a_T(XSTEPS - 2)
            a_T(XSTEPS - 1)

        @block.tensor
        def _(pe):
            pe.sem_inc(s["pv_done"], 2)
            pe.sem_inc(s["o5_done"], 2)
            pe.sem_inc(s["xt_done"], 1)
            pe.wait_ge(s["pool_c"], 1)
            pe.wait_ge(s["sc_dve"], 1)
            pe.transpose(bank(0, NB), cth[:, :], ident[0:NB, 0:NB]).then_inc(s["sc_pe"], 1)
            pe.wait_ge(s["sc_dve"], 2)
            wm = modb[:, 0:2, :, :].rearrange("p a b d -> p (a b d)")
            for j in range(2):
                pe.matmul(bank(1, NB, j * NB), wm[:, j * D:(j + 1) * D], scT[:, :], start=True, stop=True)
            pe.matmul(PS[0:NB, 2, :], scT[:, :], wm[:, 2 * D:6 * D], start=True, stop=True).then_inc(s["md_pe"], 1)
            pe.wait_ge(s["ld_b"], 64)
            pe.matmul(PS[0:H, 3, 0:RL], relb[:, :], oneh[:, :], start=True, stop=True).then_inc(s["dr_pe"], 1)
            pe.wait_ge(s["ld_w"], 16 * 11)
            pe.transpose(bank(4, NE), gate[:, :], ident[0:NE, 0:NE]).then_inc(s["gt_pe"], 1)
            pe.wait_ge(s["gt_dve"], 1)

            def x_T(b):
                pe.wait_ge(s["xh_ready"], b + 1)
                pe.wait_ge(s["qkt_act"], 2 * b + 2)
                for t in range(TPB):
                    last = pe.transpose(bank(PRE, P, t * P), XH[:, t, :], ident[:, :])
                last.then_inc(s["xt_done"], 1)

            def qkv(b, par):
                pe.wait_ge(s["hT_ready"], b + 1)
                pe.wait_ge(s["qkt_dve"], 2 * b + 2)
                for t in range(TPB):
                    pe.matmul(bank(PRE + t, 3 * D), hT[par][:, t * P:(t + 1) * P], wqkv[:, :], start=True, stop=True)
                    last = pe.matmul(bank(PRE + t, 1, 3 * D), hsq[:, t * P:(t + 1) * P], ones[:, :], start=True, stop=True)
                last.then_inc(s["qkv_done"], 1)

            def qk_T(b, qk):
                if qk == 0:
                    pe.wait_ge(s["slots_ready"], b + 1)
                    pe.wait_ge(s["qn_done"], b + 1)
                    pe.wait_ge(s["v_ready"], b + 1)
                for t in range(TPB):
                    if qk == 1:
                        pe.wait_ge(s["qkt_act" if t == 0 else "qkt_dve"], 2 * b + 1 + 2)
                    for u in range(UNITS):
                        last = pe.transpose(bank(PRE + t).bitcast(BF16)[:, u * P:(u + 1) * P],
                                            SLOTS[:, qk, t * H + 2 * u:t * H + 2 * u + 2, :].rearrange("p h s -> p (h s)"),
                                            identb[:, :])
                    last.then_inc(s["qkt_done"], 1)

            def scores(b, par, u):
                if u == 0:
                    pe.wait_ge(s["qkt_act"], 2 * b + 2 + 2)
                    pe.wait_ge(s["qkt_dve"], 2 * b + 2 + 2)
                pe.wait_ge(s["l_ready"], b * UNITS + u + 1)
                at = S_A if u % 2 == 0 else S_B
                for j in range(2):
                    r = slice(SLOT * j, SLOT * j + 6 * HD)
                    pe.matmul(bank(at + j, SEQ), QKT[par][r, 1, u, 0:P], QKT[par][r, 0, u, :], start=True, stop=True)
                    last = pe.matmul(bank(at + j, P, SEQ), QKT[par][r, 1, u, P:SEQ], QKT[par][r, 0, u, P:SEQ],
                                     start=True, stop=True)
                last.then_inc(s["qk_done"], 1)

            def products(b, par, g):
                pe.wait_ge(s["exp_done"], b * UNITS + 2 * g + 2 + 2)
                if g == 0:
                    pe.wait_ge(s["v_ready"], b + 1)
                    pe.wait_ge(s["ynt_ready"], b + 1)
                if g == 2:
                    pe.wait_ge(s["y_ready"], b + 1)
                dst = bank(CTX + g // 2, SEQ, (g % 2) * SEQ)
                for j in range(4):
                    h, pr = 4 * g + j, PR[(2 * g + j // 2) % 4]
                    o = dst[32 * j:32 * j + 32, :]
                    pe.matmul(o, V[par][:, 0, h, :], pr[:, (j % 2) * HW:(j % 2) * HW + SEQ],
                              start=True, stop=False, skip_group_check=True)
                    pe.matmul(o[:, P:SEQ], V[par][:, 1, h, :], pr[:, (j % 2) * HW + SEQ:(j % 2 + 1) * HW],
                              start=False, stop=False, skip_group_check=True)
                pe.matmul(dst[:, 0:1], V[par][:, 1, 4 * g:4 * g + 4, :].rearrange("p h d -> p (h d)"), ones[:, :],
                          start=False, stop=True, skip_group_check=True).then_inc(s["pv_done"], 1)

            def ctx_T(b):
                pe.wait_ge(s["yt_ready"], 2 * b + 2)
                for t in range(TPB):
                    for g in range(H // 4):
                        last = pe.transpose(bank(CTX + t, P, g * P), YT[:, g, t * P:(t + 1) * P], ident[:, :])
                last.then_inc(s["o2_done"], 1)

            def yn_T(b):
                pe.wait_ge(s["o3_done"], b + 1)
                for t in range(TPB):
                    last = pe.transpose(bank(CTX, P, t * P), YN[:, t, :], ident[:, :])
                last.then_inc(s["o4_done"], 1)

            def y_out(b, par):
                pe.wait_ge(s["ynt_ready"], b + 1 + 1)
                pe.wait_ge(s["hr_ready"], b + 1 + 2)
                for t in range(TPB):
                    cols = slice(t * P, (t + 1) * P)
                    pe.matmul(bank(CTX + 1, P, t * P), YNT[:, cols], wo[:, :], start=True, stop=False)
                    last = pe.matmul(bank(CTX + 1, P, t * P), hR[par][:, cols], ident[:, :], start=False, stop=True)
                last.then_inc(s["o5_done"], 1)

            def sequence(b, par, first=False, last=False):
                scores(b, par, 0)
                if not last:
                    x_T(b + 1)
                scores(b, par, 1)
                if not last:
                    qkv(b + 1, 1 - par)
                if not first:
                    ctx_T(b - 1)
                scores(b, par, 2)
                if not first:
                    yn_T(b - 1)
                scores(b, par, 3)
                if not first:
                    y_out(b - 1, 1 - par)
                products(b, par, 0)
                scores(b, par, 4)
                scores(b, par, 5)
                products(b, par, 1)
                scores(b, par, 6)
                scores(b, par, 7)
                products(b, par, 2)
                if not last:
                    qk_T(b + 1, 0)
                products(b, par, 3)
                if not last:
                    qk_T(b + 1, 1)

            x_T(0)
            qkv(0, 0)
            qk_T(0, 0)
            qk_T(0, 1)
            sequence(0, 0, first=True)
            with pe.Fori(0, (NB - 2) // 2) as two:
                b = two * 2 + 1
                sequence(b, 1)
                sequence(b + 1, 0)
            sequence(NB - 1, 1, last=True)
            ctx_T(NB - 1)
            yn_T(NB - 1)
            y_out(NB - 1, 1)

            pe.wait_ge(s["y_ready"], NB + 1)
            with pe.Fori(0, NB // 2) as two:
                b = two * 2
                for par in range(2):
                    pe.wait_ge(s["ys_staged"], b + par + 1)
                    for t in range(TPB):
                        last = pe.transpose(bank(par, P, t * P), YS[par][:, t, :], ident[:, :])
                    last.then_inc(s["m_t"], 1)
                for par in range(2):
                    pe.wait_ge(s["m_tev"], b + par + 1)
                    for ch in range(HID // P):
                        last = pe.matmul(bank(2 + 2 * par + ch // 2, SEQ, (ch % 2) * SEQ), w1s[:, ch * P:(ch + 1) * P],
                                         mT[par], start=True, stop=True)
                    last.then_inc(s["m_hid"], 1)
                for par in range(2):
                    pe.wait_ge(s["relu_act"], b + par + 1)
                    pe.wait_ge(s["relu_dve"], b + par + 1)
                    pe.wait_ge(s["z_done"], b + par + 1)
                    for t in range(TPB):
                        for ch in range(HID // P):
                            last = pe.matmul(bank(6 + par, P, t * P), hid[par][:, ch, t * P:(t + 1) * P], w2s[:, ch, :],
                                             start=(ch == 0), stop=(ch == HID // P - 1))
                    last.then_inc(s["m_z"], 1)
            with pe.Fori(0, NB // 2) as two:
                b = two * 2
                for par in range(2):
                    at = 4 * par
                    pe.wait_ge(s["h2_ready"], b + par + 1)
                    for t in range(TPB):
                        last = pe.transpose(bank(at, P, t * P), H2[par][:, t, :], ident[:, :])
                    last.then_inc(s["r_t"], 1)
                    pe.wait_ge(s["r_tev"], b + par + 1)
                    for t in range(TPB):
                        last = pe.matmul(bank(at + 1, NE, t * NE), H2T[par][:, t * P:(t + 1) * P], gateT[:, :],
                                         start=True, stop=True)
                    last.then_inc(s["r_lg"], 1)
                    pe.wait_ge(s["r_mask"], b + par + 1)
                    pe.matmul(bank(at + 2, NE), tri[:, :], maskb[:, 0, :], start=True, stop=False)
                    pe.matmul(bank(at + 2, NE), onesb[:, :], seen[:, :], start=False, stop=True)
                    pe.matmul(bank(at + 2, NE, NE), tri[:, :], maskb[:, 1, :], start=True, stop=False)
                    pe.matmul(bank(at + 2, NE, NE), onesb[:, :], maskb[:, 0, :], start=False, stop=False)
                    pe.matmul(bank(at + 2, NE, NE), onesb[:, :], seen[:, :], start=False, stop=True).then_inc(s["r_rank"], 1)
            pe.wait_ge(s["pos_ready"], NB)
            pe.matmul(bank(0, NE), onesb[:, :], seen[:, :], start=True, stop=True).then_inc(s["cnt_pe"], 1)
            pe.wait_ge(s["tv_ready"], 1)
            for j in range(4):
                last = pe.matmul(PS[0:1, 1, j * P:(j + 1) * P], tv[:, j:j + 1], ident[:, :], start=True, stop=True)
            last.then_inc(s["tv_pe"], 1)
            pe.wait_ge(s["t_ready"], 1)
            pe.wait_ge(s["ld_e"], 32)
            e_of = treg[0:1, 0:2, :].rearrange("p a b -> p (a b)")
            w2f = w2e[:, :, :].rearrange("i e d -> i (e d)")

            def rows_T(i, par, ii):
                pe.wait_ge(s[f"x_rows{par}"], 16 * XG * (ii + 1))
                pe.wait_ge(s["xt_ev"], i + 1)
                for j in range(XG):
                    last = pe.transpose(bank(par, P, j * P), xg[par][:, j * P:(j + 1) * P], ident[:, :])
                last.then_inc(s["xt_pe"], 1)

            def gate_up(i, par):
                pe.wait_ge(s["xt_ev"], i + 1 + 2)
                pe.wait_ge(s["a_dve"], i + 1)
                settle(pe)
                for j in range(XG):
                    e = pe.value_load(e_of[:, bass.ds(i * XG + j, 1)], min_val=0, max_val=NE - 1)
                    last = pe.matmul(bank(2 + 2 * par + j // 2, 2 * INNER, (j % 2) * 2 * INNER),
                                     xgT[par][:, j * P:(j + 1) * P], w13[:, bass.ds(e * (2 * INNER), 2 * INNER)],
                                     start=True, stop=True)
                last.then_inc(s["gu_pe"], 1)

            def a_T(i, par):
                pe.wait_ge(s["a_dve"], i + 1 + 2)
                for j in range(XG):
                    last = pe.transpose(PS[0:INNER, 6, j * P:(j + 1) * P], aa[par][:, j * INNER:(j + 1) * INNER], ident[:, :])
                last.then_inc(s["at_pe"], 1)

            def down(i):
                pe.wait_ge(s["at_act"], i + 1)
                pe.wait_ge(s["y_ev"], i + 1)
                settle(pe)
                for j in range(XG):
                    e = pe.value_load(e_of[:, bass.ds(i * XG + j, 1)], min_val=0, max_val=NE - 1)
                    last = pe.matmul(bank(7, P, j * P), aT[0:INNER, j * P:(j + 1) * P], w2f[:, bass.ds(e * D, D)],
                                     start=True, stop=True)
                last.then_inc(s["y_pe"], 1)

            rows_T(0, 0, 0)
            rows_T(1, 1, 0)
            gate_up(0, 0)
            with pe.Fori(0, (XSTEPS - 2) // 2) as ii:
                for par in range(2):
                    i = ii * 2 + par
                    rows_T(i + 2, par, ii + 1)
                    gate_up(i + 1, 1 - par)
                    a_T(i, par)
                    down(i)
            gate_up(XSTEPS - 1, 1)
            a_T(XSTEPS - 2, 0)
            down(XSTEPS - 2)
            a_T(XSTEPS - 1, 1)
            down(XSTEPS - 1)

        @block.vector
        def _(dve):
            st = Steps(dve, "dve_s")
            dve.sem_inc(s["qkt_dve"], 2)
            dve.sem_inc(s["l_ready"], 2)
            dve.sem_inc(s["z_done"], 2)
            dve.sem_inc(s["xt_ev"], 2)
            dve.sem_inc(s["a_dve"], 2)
            dve.sem_inc(s["y_ev"], 1)
            dve.sem_inc(s["g_free"], 2)
            for n in range(2):
                dve.sem_inc(s[f"ost{n}"], 16)
            dve.wait_ge(s["sc_act"], 1)
            st(dve.tensor_scalar(cth[:, :], cth[:, :], 0.5, 0.5, ALU.mult, ALU.add))
            st.wait()
            dve.tensor_tensor(cth[:, :], cth[:, :], csb[:, :], ALU.mult).then_inc(s["sc_dve"], 1)
            dve.wait_ge(s["sc_pe"], 1)
            dve.tensor_copy(scT[:, :], bank(0, NB)).then_inc(s["sc_dve"], 1)
            dve.wait_ge(s["md_pe"], 1)
            dve.tensor_copy(modT[:, 0:NB], bank(1, NB))
            dve.tensor_scalar(modT[:, NB:], bank(1, NB, NB), 1.0, None, ALU.add).then_inc(s["md_dve"], 1)
            st(dve.tensor_copy(mrow[:, :, :].rearrange("b m d -> b (m d)"), PS[0:NB, 2, :]))
            st.wait()
            gg = mrow[:, 0:4:3, :]
            st(dve.scalar_tensor_tensor(mtmp[:, :, :], gg, -1.0, gg, ALU.mult, ALU.max))
            st.wait()
            st(dve.tensor_scalar(mtmp[:, :, :], mtmp[:, :, :], 0.25, None, ALU.max))
            st(dve.tensor_scalar(gg, gg, 0.0, 2.0, ALU.is_ge, ALU.mult))
            st(dve.tensor_scalar(mrow[:, 2, :], mrow[:, 2, :], 1.0, None, ALU.add))
            st.wait()
            dve.scalar_tensor_tensor(gg, gg, -1.0, mtmp[:, :, :], ALU.add, ALU.mult).then_inc(s["md_dve"], 1)
            dve.wait_ge(s["dr_pe"], 1)
            dve.wait_ge(s["ld_b"], 64)
            dve.tensor_scalar(drow[:, :], PS[0:H, 3, 0:RL], scol[:, 0:1], None, ALU.mult).then_inc(s["dr_dve"], 1)
            dve.wait_ge(s["dr_dve"], 1)
            st(dve.tensor_reduce(flagf[0:H, 0:1], drow[:, :], AX_X, ALU.max, apply_absolute_value=True))
            st(dve.scalar_tensor_tensor(flagf[0:H, 1:2], scol[:, :], -1.0, scol[:, :], ALU.mult, ALU.max))
            st.wait()
            st(dve.tensor_tensor(flagf[0:H, 2:3], flagf[0:H, 0:1], flagf[0:H, 1:2], ALU.add))
            dve.memset(drow[:, 0:P], MASKED).then_inc(s["dr_dve"], 1)
            dve.wait_ge(s["ld_w"], 16 * 11)
            dve.wait_ge(s["gt_pe"], 1)
            dve.tensor_scalar(wqkv[:, :], wqkv[:, :], ln1[:, 0:1], None, ALU.mult)
            dve.tensor_scalar(w1s[:, :], w1s[:, :], ln2[:, 0:1], None, ALU.mult)
            st(dve.tensor_copy(qscale[:, :, :], srow[:, :].unsqueeze(1).to_broadcast([P, TPB, H])))
            st.wait()
            dve.memset(qscale[0:1, 0, :], 0.0)
            dve.tensor_copy(gateT[:, :], bank(4, NE)).then_inc(s["gt_dve"], 1)
            dve.wait_ge(s["pool_c"], 1)
            st(dve.memset(nt1[0:32, 0:32], 0.0))
            st.wait()
            st(dve.tensor_copy(nt1[0:H, 0:1], flagf[0:H, 2:3]))
            st.wait()
            st(dve.transpose(nt2[0:32, 0:32], nt1[0:32, 0:32]))
            st.wait()
            st(dve.tensor_reduce(flagf[0:1, 3:4], nt2[0:1, 0:32], AX_X, ALU.max))
            st.wait()
            st(dve.tensor_scalar(flagf[0:1, 3:4], flagf[0:1, 3:4], SAFE, -1.0, ALU.is_le, ALU.mult))
            st.wait()
            dve.tensor_scalar(flagi[0:1, 0:1], flagf[0:1, 3:4], 1.0, None, ALU.add).then_inc(s["flag_ready"], 1)
            dve.wait_ge(s["ld_x"], 64)
            row_stats(dve, st, X)
            mean_var(dve, st)
            st.wait()
            st(dve.tensor_scalar(var[:, :], var[:, :], LN_EPS, None, ALU.add))
            st.wait()
            rsqrt(dve, st, rstd[:, :], var[:, :], st1[:, :], st2[:, :])
            st.wait()
            dve.wait_ge(s["flag_ready"], 1)
            big = dve.value_load(flagi[0:1, 0:1], min_val=0, max_val=1)
            dve.wait_ge(s["ld_bias"], 16 * 2 * H)
            dve.memset(BIAS[:, :, 0:HW + 1:HW], 0.0).then_inc(s["bias0"], 1)
            dve.wait_ge(s["bias0"], 1)
            base = st.n
            STEPS_B = 21

            def x_hat(b):
                dve.wait_ge(s["xt_done"], b + 1)
                for t in range(TPB):
                    last = dve.tensor_scalar(XH[:, t, :], tok1(X, b, t), mean[:, bass.ds(b * TPB + t, 1)],
                                             rstd[:, bass.ds(b * TPB + t, 1)], ALU.subtract, ALU.mult)
                last.then_inc(s["xh_ready"], 1)

            def norms(b):
                step = Steps(dve, "dve_s")
                step.at = b * STEPS_B + base
                nqk = 2 * TPB * H
                dve.wait_ge(s["sq_done"], b + 1)
                step(dve.tensor_reduce(nt1[:, 0:nqk], sq[:, :].rearrange("p (n d) -> p n d", d=HD), AX_X, ALU.add))
                step(dve.tensor_scalar(arg[:, nqk:], PS[:, PRE:PRE + TPB, 3 * D], 1.0 / D, RMS_EPS, ALU.mult, ALU.add))
                step.wait()
                step(dve.tensor_scalar(em[:, :], arg[:, nqk:], KQ_EPS, None, ALU.mult))
                step.wait()
                for qk in range(2):
                    sl = slice(qk * TPB * H, (qk + 1) * TPB * H)
                    last = dve.tensor_tensor(arg[:, sl].rearrange("p (t h) -> p t h", t=TPB),
                                             nt1[:, sl].rearrange("p (t h) -> p t h", t=TPB),
                                             em[:, :].unsqueeze(2).to_broadcast([P, TPB, H]), ALU.add)
                step(last)
                step.wait()
                last = rsqrt(dve, step, rs[:, :], arg[:, :], nt1[:, :], nt2[:, :])
                step.wait()
                dve.tensor_tensor(rs[:, 0:TPB * H], rs[:, 0:TPB * H], qscale[:, :, :].rearrange("p t h -> p (t h)"),
                                  ALU.mult).then_inc(s["rs_done"], 1)
                dve.wait_ge(s["rs_done"], b + 1)
                for t in range(TPB):
                    last = dve.tensor_tensor(
                        QKN[:, :].rearrange("p (q t h d) -> p q t h d", q=2, t=TPB, h=H)[:, :, t, :, :],
                        bank(PRE + t, 2 * D).rearrange("p (q h d) -> p q h d", q=2, h=H),
                        rs[:, 0:nqk].rearrange("p (q t h) -> p q t h", q=2, t=TPB)[:, :, t, :].unsqueeze(3)
                        .to_broadcast([P, 2, H, HD]), ALU.mult)
                last.then_inc(s["qn_done"], 1)
                step.n += 3
                assert step.n == STEPS_B, step.n

            def split(b):
                step = Steps(dve, "dve_s")
                step.at = b * STEPS_B + base
                step.n = STEPS_B - 3
                flat = [p_[:, :, :, :].rearrange("p q h d -> p (q h d)") for p_ in part]
                dve.wait_ge(s["qn_done"], b + 1)
                step(dve.tensor_copy(flat[0], QKN[:, :]))
                step.wait()
                step(dve.tensor_tensor(QKR[:, :], QKN[:, :], flat[0], ALU.subtract))
                step.wait()
                step(dve.tensor_copy(flat[1], QKR[:, :]))
                step.wait()
                dve.tensor_tensor(flat[2], QKR[:, :], flat[1], ALU.subtract).then_inc(s["split_done"], 1)

            def qk_half(b, par, qk):
                dve.wait_ge(s["qkt_done"], b * 4 + 2 * qk + 2)
                dve.tensor_copy(QKT[par][:, qk, :, P:SEQ], bank(PRE + 1).bitcast(BF16).rearrange("p (u t) -> p u t", u=UNITS)
                                ).then_inc(s["qkt_dve"], 1)

            def add(b, u):
                dve.wait_ge(s["qk_done"], b * UNITS + u + 1)
                dve.wait_ge(s["exp_done"], b * UNITS + u + 1)
                settle(dve)
                at = S_A if u % 2 == 0 else S_B

                def plus_bias():
                    return dve.tensor_tensor(L[u % 2][:, :].rearrange("p (j w) -> p j w", j=2), PS[:, at:at + 2, 0:HW],
                                             BIAS[:, u, :].rearrange("p (j w) -> p j w", j=2), ALU.add)
                with dve.If(big == 1):
                    plus_bias().then_inc(s["g_in"], 1)
                    dve.wait_ge(s["g_max"], b * UNITS + u + 1)
                    m = LM[:, :].rearrange("p (j w) -> p j w", j=2)
                    v = L[u % 2][:, :].rearrange("p (j w) -> p j w", j=2)
                    dve.tensor_tensor(m[:, :, P:SEQ], m[:, :, P:SEQ], m[:, :, SEQ:], ALU.max).then_inc(s["g_dve"], 1)
                    dve.wait_ge(s["g_dve"], b * UNITS + u + 1)
                    dve.tensor_tensor(v[:, :, 0:SEQ], v[:, :, 0:SEQ], m[:, :, 0:SEQ], ALU.subtract)
                    dve.tensor_tensor(v[:, :, SEQ:], v[:, :, SEQ:], m[:, :, P:SEQ], ALU.subtract).then_inc(s["l_ready"], 1)
                with dve.Else():
                    plus_bias().then_inc(s["l_ready"], 1)

            def normalize(b):
                dve.wait_ge(s["o2_done"], b + 1)
                v = PS[:, CTX:CTX + TPB, :].rearrange("p t (h s) -> p t h s", s=32)
                dve.reciprocal(rden[:, :, :], v[:, :, :, HD]).then_inc(s["c_s"], 1)
                dve.wait_ge(s["c_s"], b + 1)
                dve.tensor_tensor(YN[:, :, :].rearrange("p t (h d) -> p t h d", d=HD), v[:, :, :, 0:HD],
                                  rden[:, :, :].unsqueeze(3).to_broadcast([P, TPB, H, HD]), ALU.mult).then_inc(s["o3_done"], 1)

            def sequence(b, par, first=False, last=False):
                if not last:
                    x_hat(b + 1)
                add(b, 0)
                add(b, 1)
                if not first:
                    normalize(b - 1)
                add(b, 2)
                if not last:
                    norms(b + 1)
                add(b, 3)
                if not last:
                    split(b + 1)
                for u in range(4, UNITS):
                    add(b, u)
                if not last:
                    qk_half(b + 1, 1 - par, 0)
                    qk_half(b + 1, 1 - par, 1)

            x_hat(0)
            norms(0)
            split(0)
            qk_half(0, 0, 0)
            qk_half(0, 0, 1)
            sequence(0, 0, first=True)
            with dve.Fori(0, (NB - 2) // 2) as two:
                b = two * 2 + 1
                sequence(b, 1)
                sequence(b + 1, 0)
            sequence(NB - 1, 1, last=True)
            normalize(NB - 1)
            st.n = base + NB * STEPS_B

            dve.wait_ge(s["y_ready"], NB + 1)
            row_stats(dve, st, Y)
            mean_var(dve, st)
            st.wait()
            st(dve.tensor_tensor(st1[:, :], mean[:, :], mean[:, :], ALU.mult))
            st.wait()
            st(dve.scalar_tensor_tensor(var[:, :], st1[:, :], RMS_EPS, var[:, :], ALU.add, ALU.add))
            st.wait()
            rsqrt(dve, st, rstd[:, :], var[:, :], st1[:, :], st2[:, :])
            st.wait()
            dve.wait_ge(s["ld_mod"], 16)
            base_m = st.n
            with dve.Fori(0, NB // 2) as two:
                b = two * 2
                step = Steps(dve, "dve_s")
                step.at = b * 2 + base_m
                for par in range(2):
                    dve.tensor_scalar(YS[par], tok(Y, b + par, 0, TPB), 0.0, None, ALU.add).then_inc(s["ys_staged"], 1)
                for par in range(2):
                    dve.wait_ge(s["m_hid"], b + par + 1)
                    dve.tensor_scalar(hid[par][:, 2:4, :].rearrange("p c t -> p (c t)"), bank(3 + 2 * par), 0.0, None,
                                      ALU.max).then_inc(s["relu_dve"], 1)
                for par in range(2):
                    dve.wait_ge(s["m_z"], b + par + 1)
                    for t in range(TPB):
                        last = dve.scalar_tensor_tensor(zt[:, t, :], bank(6 + par, P, t * P),
                                                        rstd[:, bass.ds((b + par) * TPB + t, 1)], YS[par][:, t, :],
                                                        ALU.mult, ALU.add)
                    last.then_inc(s["z_done"], 1)
                    dve.wait_ge(s["z_done"], b + par + 1 + 2)
                    step(dve.tensor_tensor(zt[:, :, :], zt[:, :, :], modb[:, bass.ds(b + par, 1), 0, :].to_broadcast([P, TPB, D]),
                                           ALU.mult))
                    step.wait()
                    step(dve.tensor_tensor(tok(X, b + par, 0, TPB), tok(X, b + par, 0, TPB), zt[:, :, :], ALU.add))
                    step.wait()
            st.n = base_m + 2 * NB
            dve.memset(zeros, 0.0).then_inc(s["zero_ready"], 1)
            row_stats(dve, st, X)
            mean_var(dve, st)
            st.wait()
            st(dve.tensor_scalar(var[:, :], var[:, :], LN_EPS, None, ALU.add))
            st.wait()
            rsqrt(dve, st, rstd[:, :], var[:, :], st1[:, :], st2[:, :])
            st.wait()
            base_r = st.n
            STEPS_R = 12
            def route(b, par, before=None):
                step = Steps(dve, "dve_s")
                step.at = b * STEPS_R + base_r
                if before is not None:
                    dve.wait_ge(s[f"scat{par}"], before * (TPB * TOPK * 16))
                for t in range(TPB):
                    last = dve.tensor_scalar(H2[par][:, t, :], tok1(X, b, t), mean[:, bass.ds(b * TPB + t, 1)],
                                             rstd[:, bass.ds(b * TPB + t, 1)], ALU.subtract, ALU.mult)
                step(last)
                step.wait()
                step(dve.tensor_tensor(H2[par], H2[par], modb[:, bass.ds(b, 1), 2, :].to_broadcast([P, TPB, D]), ALU.mult))
                step.wait()
                dve.tensor_tensor(H2[par], H2[par], modb[:, bass.ds(b, 1), 1, :].to_broadcast([P, TPB, D]),
                                  ALU.add).then_inc(s["h2_ready"], 1)
                dve.wait_ge(s["r_th"], b + 1)
                step(dve.tensor_scalar(score[:, :, :], th[:, :, :], 0.5, 0.5, ALU.mult, ALU.add))
                step.wait()
                step(dve.tensor_tensor(sel[:, :, :], score[:, :, :], ebias[:, :].unsqueeze(1).to_broadcast([P, TPB, NE]), ALU.add))
                step.wait()
                settle(dve)
                for t in range(TPB):
                    last = dve.max(top[:, t, :], sel[:, t, :])
                step(last)
                step.wait()
                settle(dve)
                for t in range(TPB):
                    last = dve.max_index(topi[:, t, :], top[:, t, :], sel[:, t, :])
                step(last)
                step.wait()
                ids = nt1[:, 0:TPB * TOPK]
                step(dve.tensor_copy(ids.rearrange("p (t k) -> p t k", t=TPB), topi[:, :, 0:TOPK]))
                step.wait()
                oh = OH[:, :, :, :].rearrange("p t k e -> p (t k) e")
                oht = OHT[:, :, :, :].rearrange("p t k e -> p (t k) e")
                step(dve.tensor_tensor(oh, iota_e[:, :].unsqueeze(1).to_broadcast([P, TPB * TOPK, NE]),
                                       ids.unsqueeze(2).to_broadcast([P, TPB * TOPK, NE]), ALU.is_equal))
                step.wait()
                dve.tensor_reduce(maskb[:, :, :], OH[:, :, :, :].rearrange("p t k e -> p t e k"), AX_X, ALU.max
                                  ).then_inc(s["r_mask"], 1)
                dve.tensor_scalar(IDX[:, bass.ds(b * TPB * TOPK, TPB * TOPK)], ids, 0.0, None, ALU.add)
                step(dve.tensor_tensor(OHT[:, :, :, :], OH[:, :, :, :],
                                       score[:, :, :].unsqueeze(2).to_broadcast([P, TPB, TOPK, NE]), ALU.mult))
                step.wait()
                step(dve.tensor_reduce(rk[:, :], oht, AX_X, ALU.add))
                step.wait()
                step(dve.tensor_reduce(wsum[:, :], rk[:, :].rearrange("p (t k) -> p t k", t=TPB), AX_X, ALU.add))
                step.wait()
                step(dve.reciprocal(wsum[:, :], wsum[:, :]))
                step.wait()
                dve.tensor_tensor(WT[:, bass.ds(b * TPB * TOPK, TPB * TOPK)].rearrange("p (t k) -> p t k", t=TPB),
                                  rk[:, :].rearrange("p (t k) -> p t k", t=TPB),
                                  wsum[:, :].unsqueeze(2).to_broadcast([P, TPB, TOPK]), ALU.mult)
                dve.wait_ge(s["r_rank"], b + 1)
                dve.tensor_tensor(OHT[:, :, :, :], OH[:, :, :, :],
                                  bank(4 * par + 2, TPB * NE).rearrange("p (t e) -> p t e", t=TPB).unsqueeze(2)
                                  .to_broadcast([P, TPB, TOPK, NE]), ALU.mult).then_inc(s["r_s"], 1)
                dve.tensor_tensor(seen[:, :], seen[:, :], maskb[:, 0, :], ALU.add).then_inc(s["r_s"], 1)
                dve.wait_ge(s["r_s"], b * 3 + 2)
                dve.tensor_tensor(seen[:, :], seen[:, :], maskb[:, 1, :], ALU.add)
                dve.tensor_reduce(rk[:, :], oht, AX_X, ALU.add).then_inc(s["r_s"], 1)
                dve.wait_ge(s["r_s"], b * 3 + 3)
                dve.tensor_scalar(RK[:, bass.ds(b * TPB * TOPK, TPB * TOPK)], rk[:, :], 0.0, None, ALU.add)
                dve.scalar_tensor_tensor(posi[par][:, :], ids, float(REGION), rk[:, :], ALU.mult, ALU.add
                                         ).then_inc(s["pos_ready"], 1)
                assert step.n == STEPS_R, step.n

            for par in range(2):
                route(par, par)
            with dve.Fori(1, NB // 2) as two:
                for par in range(2):
                    route(two * 2 + par, par, before=two)
            st.n = base_r + NB * STEPS_R

            dve.wait_ge(s["cnt_pe"], 1)
            st(dve.tensor_copy(cnt[:, :], bank(0, NE)))
            st.wait()
            dve.scalar_tensor_tensor(rowi[:, :], iota_e[0:1, :], float(REGION), cnt[0:1, :], ALU.mult, ALU.add
                                     ).then_inc(s["rows_ready"], 1)
            st(dve.tensor_scalar(cnti[:, :], cnt[:, :], float(P - 1), None, ALU.add))
            st.wait()
            st(dve.tensor_scalar(cnti[:, :], cnti[:, :], 7, None, ALU.logical_shift_right))
            st.wait()
            st(dve.tensor_copy(ntile[:, :], cnti[:, :]))
            st.wait()
            st(dve.tensor_tensor_scan(tend[:, :], onesf[:, :], ntile[:, :], 0.0, ALU.mult, ALU.add))
            st.wait()
            st(dve.tensor_tensor(tstart[:, :], tend[:, :], ntile[:, :], ALU.subtract))
            for j in range(2):
                last = dve.tensor_scalar(ge[:, j, :], tend[:, :], tile_no[:, j:j + 1], None, ALU.is_le)
            st(last)
            st.wait()
            st(dve.tensor_tensor(ge2[:, :, :], ge[:, :, :], ntile[:, :].unsqueeze(1).to_broadcast([P, 2, NE]), ALU.mult))
            st(dve.tensor_reduce(tv[:, 0:2], ge[:, :, :], AX_X, ALU.add))
            st.wait()
            st(dve.tensor_reduce(tv[:, 2:4], ge2[:, :, :], AX_X, ALU.add))
            st(dve.tensor_scalar(nt1[:, 0:2], tv[:, 0:2], NE - 0.5, float(P), ALU.is_lt, ALU.mult))
            st.wait()
            st(dve.tensor_tensor(nt2[:, 0:2], tile_no[:, :], tv[:, 2:4], ALU.subtract))
            st.wait()
            st(dve.tensor_tensor(nt2[:, 0:2], nt2[:, 0:2], nt1[:, 0:2], ALU.mult))
            st.wait()
            st(dve.scalar_tensor_tensor(tv[:, 2:4], tv[:, 0:2], float(REGION), nt2[:, 0:2], ALU.mult, ALU.add))
            st.wait()
            dve.tensor_scalar(tv[:, 0:2], tv[:, 0:2], float(NE - 1), None, ALU.min).then_inc(s["tv_ready"], 1)
            dve.wait_ge(s["tv_pe"], 1)
            dve.tensor_copy(treg[:, :, :].rearrange("p a b -> p (a b)"), PS[0:1, 1, :]).then_inc(s["t_ready"], 1)
            NPK = NT * TOPK // 4
            big3 = BIG[:, :].rearrange("p (n e) -> p n e", e=NE)
            for q in range(4):
                cs = slice(q * NPK, (q + 1) * NPK)
                st(dve.tensor_tensor(big3, iota_e[:, :].unsqueeze(1).to_broadcast([P, NPK, NE]),
                                     IDX[:, cs].unsqueeze(2).to_broadcast([P, NPK, NE]), ALU.is_equal))
                st.wait()
                st(dve.tensor_tensor(big3, big3, tstart[:, :].unsqueeze(1).to_broadcast([P, NPK, NE]), ALU.mult))
                st.wait()
                st(dve.tensor_reduce(IDX[:, cs], big3, AX_X, ALU.add))
                st.wait()
                last = dve.scalar_tensor_tensor(POS[:, cs], IDX[:, cs], float(P), RK[:, cs], ALU.mult, ALU.add)
            last.then_inc(s["pos_all"], 1)

            def rows_ev(i, par):
                dve.wait_ge(s["xt_pe"], i + 1)
                dve.tensor_copy(xgT[par], bank(par)).then_inc(s["xt_ev"], 1)

            def act_mul(i, par):
                dve.wait_ge(s["sg_act"], i + 1)
                dve.tensor_tensor(aa[par].rearrange("p (a b i) -> p a b i", a=2, b=2),
                                  sg[par].rearrange("p (a b i) -> p a b i", a=2, b=2),
                                  PS[:, 2 + 2 * par:4 + 2 * par, 0:4 * INNER]
                                  .rearrange("p a (b g i) -> p a b g i", b=2, g=2)[:, :, :, 1, :],
                                  ALU.mult).then_inc(s["a_dve"], 1)

            def y_evac(i, par, ii):
                dve.wait_ge(s["y_pe"], i + 1)
                if ii is not None:
                    dve.wait_ge(s[f"yst{par}"], 16 * ii)
                dve.tensor_copy(yo[par], bank(7)).then_inc(s["y_ev"], 1)

            rows_ev(0, 0)
            rows_ev(1, 1)
            act_mul(0, 0)
            rows_ev(2, 0)
            act_mul(1, 1)
            y_evac(0, 0, None)
            rows_ev(3, 1)
            act_mul(2, 0)
            y_evac(1, 1, None)
            with dve.Fori(1, (XSTEPS - 2) // 2) as ii:
                for par in range(2):
                    i = ii * 2 + par
                    rows_ev(i + 2, par)
                    act_mul(i + 1, 1 - par)
                    y_evac(i, par, ii)
            act_mul(XSTEPS - 1, 1)
            y_evac(XSTEPS - 2, 0, XSTEPS // 2 - 1)
            y_evac(XSTEPS - 1, 1, XSTEPS // 2 - 1)

            with dve.Fori(0, NT // 2) as two:
                n2 = two * 2
                for par in range(2):
                    n = n2 + par
                    dve.wait_ge(s[f"gsem{par}"], n2 * (TOPK * 8) + 16 * TOPK)
                    dve.wait_ge(s[f"ost{par}"], n2 * 8 + 16)
                    dve.tensor_scalar(acc[par][:, :], G[par][:, 0, :], WT[:, bass.ds(n * TOPK, 1)], None, ALU.mult
                                      ).then_inc(s["acc_s"], 1)
                    for k in range(1, TOPK):
                        dve.wait_ge(s["acc_s"], n * 5 + k)
                        dve.scalar_tensor_tensor(acc[par][:, :], G[par][:, k, :], WT[:, bass.ds(n * TOPK + k, 1)],
                                                 acc[par][:, :], ALU.mult, ALU.add).then_inc(s["acc_s"], 1)
                    dve.wait_ge(s["acc_s"], n * 5 + 4)
                    dve.sem_inc(s["g_free"], 1)
                    dve.tensor_tensor(acc[par][:, :], acc[par][:, :],
                                      modb[:, bass.ds(n // TPB, 1), 3, :].rearrange("p a d -> p (a d)"), ALU.mult
                                      ).then_inc(s["acc_s"], 1)
                    dve.wait_ge(s["acc_s"], n * 5 + 5)
                    dve.tensor_tensor(acc[par][:, :], acc[par][:, :],
                                      X[:, bass.ds(n, 1), :].rearrange("p a d -> p (a d)"), ALU.add
                                      ).then_inc(s["acc_ready"], 1)


NAMES = ["x", "ln1_w", "Wq", "Wk", "Wv", "rel_bias", "scale", "Wo", "ln2_w", "W1", "W2", "gate_w", "w1", "w3", "w2",
         "e_bias", "c", "wmod"]


def kernel(L0_attn_x, L0_attn_ln1_w, L0_attn_Wq, L0_attn_Wk, L0_attn_Wv, L0_attn_rel_bias, L0_attn_scale,
           L0_attn_Wo, L0_attn_ln2_w, L0_attn_W1, L0_attn_W2, L0_ffn_gate_w, L0_ffn_w1, L0_ffn_w3, L0_ffn_w2,
           L0_ffn_e_bias, L0_c, L0_wmod):
    import concourse.bacc as bacc
    from concourse.bass_utils import run_bass_kernel_spmd

    values = [L0_attn_x, L0_attn_ln1_w, L0_attn_Wq, L0_attn_Wk, L0_attn_Wv, L0_attn_rel_bias, L0_attn_scale,
              L0_attn_Wo, L0_attn_ln2_w, L0_attn_W1, L0_attn_W2, L0_ffn_gate_w, L0_ffn_w1, L0_ffn_w3, L0_ffn_w2,
              L0_ffn_e_bias, L0_c, L0_wmod, bucket_one_hot()]
    nc = bacc.Bacc("TRN2", target_bir_lowering=False, num_devices=1)
    arrays, args = {}, []
    for name, value in zip(NAMES + ["onehot"], values):
        a = np.ascontiguousarray(value)
        arrays[f"in_{name}"] = a
        args.append(nc.dram_tensor(f"in_{name}", a.shape, mybir.dt.from_np(a.dtype), kind="ExternalInput").ap())
    out = nc.dram_tensor("out", (NB, SEQ, D), F32, kind="ExternalOutput").ap()
    build(nc, *args, out)
    r = run_bass_kernel_spmd(nc, [arrays], core_ids=[0])
    return r.results[0]["out"]
```

```python
from contextlib import ExitStack

import numpy as np
import concourse.bass as bass
from concourse import mybir

ALU = mybir.AluOpType
ACT = mybir.ActivationFunctionType
F32 = mybir.dt.float32
BF16 = mybir.dt.bfloat16
I32 = mybir.dt.int32
U32 = mybir.dt.uint32
AX_X = mybir.AxisListType.X
RMAX = bass.bass_isa.ReduceOp.max

P = 128
NB, SEQ, D = 16, 256, 128
TPB = SEQ // P
NT = NB * TPB
H, HD = 16, 8
HID = 512
NBUCKET, MAXDIST = 32, 128
NE, TOPK, INNER = 32, 4, 96
LN_EPS, RMS_EPS, KQ_EPS = 1e-5, 1e-6, 1e-6
MASKED = -1e30
SAFE = 80.0
RL = 3 * P
UNITS = H // 2
HW = SEQ + P
UW = 2 * HW
SLOT = 64
REGION = NB * SEQ + P
DUMMY = NE * REGION
XTILES = NT * TOPK + NE
XG = 4
XSTEPS = XTILES // XG
GROUP = 4
S_A, S_B = 0, 2
PRE, CTX = 4, 6


def bucket_one_hot():
    out = np.zeros((NBUCKET, RL), np.float32)
    exact = NBUCKET // 2
    for d in range(1, SEQ):
        if d < exact:
            n = d
        else:
            big = np.log(np.float32(d) / np.float32(exact)) / np.float32(np.log(MAXDIST / exact))
            n = min(exact + int(np.float32(big * np.float32(NBUCKET - exact))), NBUCKET - 1)
        out[n, d + P - 1] = 1.0
    return out


def build(nc, x, ln1_w, Wq, Wk, Wv, rel_bias, scale, Wo, ln2_w, W1, W2, gate_w, w1, w3, w2, e_bias, c, wmod,
          onehot, out):
    ctx = ExitStack()
    with ctx:
        def sb(name, shape, dt=F32):
            return ctx.enter_context(nc.sbuf_tensor(name, shape, dt))

        def sem(name):
            return ctx.enter_context(nc.semaphore(name))

        def dram(name, shape):
            return nc.dram_tensor(name, shape, F32, kind="Internal").ap()

        mod_rows = dram("mod_rows", (NB, 4 * D))
        dist_row = dram("dist_row", (H, RL))
        dist_rep = dram("dist_rep", (H, P, RL))
        xs = dram("xs", (DUMMY + P, D))
        ys = dram("ys", (XTILES * P, D))

        ident = sb("ident", [P, P])
        identb = sb("identb", [P, P], BF16)
        tri = sb("tri", [P, P], BF16)
        onesb = sb("onesb", [P, P], BF16)
        ones = sb("ones", [P, 1])
        iota_e = sb("iota_e", [P, NE])
        tile_no = sb("tile_no", [P, 2])
        wqkv = sb("wqkv", [P, 3 * D])
        wo = sb("wo", [P, D])
        w1s = sb("w1s", [P, HID])
        w2s = sb("w2s", [P, HID // P, D])
        ln1 = sb("ln1", [P, 1])
        ln2 = sb("ln2", [P, 1])
        gate = sb("gate", [NE, D])
        gateT = sb("gateT", [P, NE])
        ebias = sb("ebias", [P, NE])
        srow = sb("srow", [P, H])
        scol = sb("scol", [H, 1])
        qscale = sb("qscale", [P, TPB, H])
        csb = sb("csb", [NB, D])
        cth = sb("cth", [NB, D])
        scT = sb("scT", [P, NB])
        modT = sb("modT", [P, 2 * NB])
        relb = sb("relb", [NBUCKET, H])
        flagf = sb("flagf", [P, 4])
        flagi = sb("flagi", [1, 4], I32)
        modb = sb("modb", [P, NB, 4, D])
        X = sb("X", [P, NT, D])
        Y = sb("Y", [P, NT, D])
        BIAS = sb("BIAS", [P, UNITS, UW])
        w13 = BIAS[:, :, :].rearrange("p u w -> p (u w)")
        w2e = sb("w2e", [INNER, NE, D])
        stats = sb("stats", [P, NT, 6])
        mean = sb("mean", [P, NT])
        var = sb("var", [P, NT])
        rstd = sb("rstd", [P, NT])
        st1 = sb("st1", [P, NT])
        st2 = sb("st2", [P, NT])
        XH = sb("XH", [P, TPB, D])
        hT = [sb(f"hT{i}", [P, SEQ]) for i in range(2)]
        hR = [sb(f"hR{i}", [P, SEQ]) for i in range(2)]
        hsq = sb("hsq", [P, SEQ])
        QKN = sb("QKN", [P, 2 * TPB * P])
        QKR = sb("QKR", [P, 2 * TPB * P])
        sq = QKR
        SLOTS = sb("SLOTS", [P, 2, TPB * H, SLOT], BF16)
        QKT = [sb(f"QKT{i}", [P, 2, UNITS, SEQ], BF16) for i in range(2)]
        V = [sb(f"V{i}", [P, TPB, H, 32]) for i in range(2)]
        NARG = 2 * TPB * H + TPB
        arg = sb("arg", [P, NARG])
        rs = sb("rs", [P, NARG])
        nt1 = sb("nt1", [P, NARG])
        nt2 = sb("nt2", [P, NARG])
        em = sb("em", [P, TPB])
        L = [sb(f"L{i}", [P, UW]) for i in range(2)]
        LM = sb("LM", [P, UW])
        PR = [sb(f"PR{i}", [P, UW]) for i in range(4)]
        YT = sb("YT", [P, H // 4, SEQ])
        rden = sb("rden", [P, TPB, H])
        YN = sb("YN", [P, TPB, D])
        YNT = sb("YNT", [P, SEQ])
        mT = [YT[:, 2 * i, :] for i in range(2)]
        YS = [YT[:, 2 * i + 1, :].rearrange("p (t d) -> p t d", t=TPB) for i in range(2)]
        hid = [sb(f"hid{i}", [P, HID // P, SEQ]) for i in range(2)]
        zt = XH
        hid_flat = [hid[i][:, :, :].rearrange("p c t -> p (c t)") for i in range(2)]
        mrow = hid_flat[1][0:NB, 0:4 * D].rearrange("b (m d) -> b m d", m=4)
        mtmp = hid_flat[1][0:NB, 4 * D:6 * D].rearrange("b (m d) -> b m d", m=2)
        oneh = hid_flat[0][0:NBUCKET, 0:RL]
        drow = hid_flat[0][0:H, RL:2 * RL]
        H2 = [PR[i][:, 0:SEQ].rearrange("p (t d) -> p t d", t=TPB) for i in range(GROUP)]
        H2T = [PR[i][:, SEQ:2 * SEQ] for i in range(2)]
        th = sb("th", [P, TPB, NE])
        score = sb("score", [P, TPB, NE])
        sel = sb("sel", [P, TPB, NE])
        top = sb("top", [P, TPB, 8])
        topi = sb("topi", [P, TPB, 8], U32)
        OH = sb("OH", [P, TPB, TOPK, NE])
        OHT = sb("OHT", [P, TPB, TOPK, NE])
        maskb = sb("maskb", [P, TPB, NE], BF16)
        seen = sb("seen", [P, NE], BF16)
        rank = sb("rank", [P, TPB, NE])
        rk = sb("rk", [P, TPB * TOPK])
        wsum = sb("wsum", [P, TPB])
        posi = [sb(f"posi{i}", [P, TPB * TOPK], I32) for i in range(GROUP)]
        mean_g = sb("mean_g", [P, GROUP * TPB])
        rstd_g = sb("rstd_g", [P, GROUP * TPB])
        var_g = sb("var_g", [P, GROUP * TPB])
        tg = [sb(f"tg{i}", [P, GROUP * TPB]) for i in range(3)]
        IDX = sb("IDX", [P, NT * TOPK])
        RK = sb("RK", [P, NT * TOPK])
        WT = sb("WT", [P, NT * TOPK])
        cnt = sb("cnt", [P, NE])
        cnti = sb("cnti", [P, NE], I32)
        ntile = sb("ntile", [P, NE])
        tend = sb("tend", [P, NE])
        tstart = sb("tstart", [P, NE])
        onesf = sb("onesf", [P, NE])
        ge = sb("ge", [P, 2, NE])
        ge2 = sb("ge2", [P, 2, NE])
        tv = sb("tv", [P, 4])
        treg = sb("treg", [1, 4, P], I32)
        rowi = sb("rowi", [1, NE], I32)
        POS = sb("POS", [P, NT * TOPK], I32)
        BIG = V[0][:, :, :, :].rearrange("p t h s -> p (t h s)")
        zeros = L[0][:, 0:P]
        xg = [PR[i][:, 0:XG * P] for i in range(4)]
        xgT = [V[1][:, i, :, :].rearrange("p h s -> p (h s)") for i in range(2)]
        sg = [L[i][:, 0:XG * INNER] for i in range(2)]
        aa = [QKN[:, 0:XG * INNER], QKR[:, 0:XG * INNER]]
        aT = [hid[1][:, 0:2, :].rearrange("p a b -> p (a b)"), YT[:, 2:4, :].rearrange("p a b -> p (a b)")]
        yo = [hid[1][:, 2:4, :].rearrange("p a b -> p (a b)"), YT[:, 0:2, :].rearrange("p a b -> p (a b)")]
        gidx = [sb(f"gidx{i}", [P, TOPK], I32) for i in range(2)]
        G = [SLOTS[:, i, :, :].rearrange("p a b -> p (a b)").bitcast(F32)[:, 0:TOPK * D]
             .rearrange("p (k d) -> p k d", k=TOPK) for i in range(2)]
        acc = [sb(f"acc{i}", [P, D]) for i in range(2)]

        PS = ctx.enter_context(nc.psum_tensor("PS", [P, 8, 512], F32))

        names = """ld_c ld_x ld_w ld_b ld_e pool_c pool_s pool_n 
            sc_act sc_dve sc_pe md_pe md_dve wr_mod ld_mod gt_pe gt_dve dr_pe dr_dve wr_dist rep_dist ld_bias bias0
            dve_s flag_ready x_stats
            xh_ready xt_done hT_ready qkv_done sq_done ss_ready rs_done v_ready qn_done parts slots_ready qkt_done
            qkt_act qkt_dve qk_done l_ready g_max g_in g_dve exp_done pv_done yt_ready o2_done o3_done o4_done
            ynt_ready o5_done y_ready
            c_s ys_staged m_t m_tev m_hid relu_act relu_dve m_z z_done 
            m_s h_s rt_s rg_s h2_free h2_ready r_t r_tev r_lg r_th r_mask r_rank  pos_ready
             cnt_pe zero_ready zero_done  x_rows0 x_rows1 x_rows2 x_rows3  tv_pe tv_ready rows_ready t_ready 
            xt_pe xt_ev gu_pe sg_act a_dve at_pe at_act y_pe y_ev yst y_free pos_all settled hr_ready
             gsem0 gsem1 acc_s acc_ready g_free ost0 ost1  scat0 scat1 pool_g""".split()
        s = {n: sem(n) for n in names}
        block = ctx.enter_context(nc.Block())

        def bank(b, n=512, m=0):
            return PS[:, b, m:m + n]

        def settle(eng):
            eng.sem_inc(s["settled"], 1)

        class Steps:
            def __init__(self, eng, name, start=0, alone=False):
                self.eng, self.sem, self.n, self.at, self.alone = eng, s[name], start, 0, alone

            def __call__(self, ins):
                ins.then_inc(self.sem, 1)
                self.n += 1
                return ins

            def wait(self):
                self.eng.wait_ge(self.sem, self.at + self.n)
                if self.alone:
                    settle(self.eng)

        def rsqrt(eng, step, y, a, t1, t2, fused=True):
            step(eng.tensor_scalar(y.bitcast(I32), a.bitcast(I32), -0.5, float(0x5f3759df), ALU.mult, ALU.add))
            for _ in range(3):
                step.wait()
                step(eng.tensor_tensor(t1, y, y, ALU.mult))
                step.wait()
                if fused:
                    step(eng.scalar_tensor_tensor(t2, t1, -0.5, a, ALU.mult, ALU.mult))
                    step.wait()
                    last = step(eng.scalar_tensor_tensor(y, t2, 1.5, y, ALU.add, ALU.mult))
                else:
                    step(eng.tensor_tensor(t2, t1, a, ALU.mult))
                    step.wait()
                    step(eng.tensor_scalar(t1, t2, -0.5, 1.5, ALU.mult, ALU.add))
                    step.wait()
                    last = step(eng.tensor_tensor(y, y, t1, ALU.mult))
            return last

        def mean_var(dve, step, n=NT, mean=mean, var=var, tmp=rstd, st1=st1, st2=st2):
            step.wait()
            step(dve.tensor_tensor(st1[:, 0:n], stats[:, 0:n, 1], stats[:, 0:n, 4], ALU.add))
            step(dve.tensor_tensor(st2[:, 0:n], stats[:, 0:n, 1], stats[:, 0:n, 4], ALU.subtract))
            step(dve.tensor_tensor(tmp[:, 0:n], stats[:, 0:n, 2], stats[:, 0:n, 5], ALU.add))
            step.wait()
            step(dve.tensor_scalar(mean[:, 0:n], st1[:, 0:n], 0.5, None, ALU.mult))
            step(dve.scalar_tensor_tensor(st2[:, 0:n], st2[:, 0:n], 0.25, st2[:, 0:n], ALU.mult, ALU.mult))
            step.wait()
            step(dve.scalar_tensor_tensor(var[:, 0:n], tmp[:, 0:n], 1.0 / D, st2[:, 0:n], ALU.mult, ALU.add))

        def load_many(engine, table, at, top, n=8):
            return nc.values_load_multi_w_load_instructions(table[:, bass.ds(at, n)], engines=[engine], min_val=0,
                                                            max_val=top)[1]

        def pad_zeros(eng, engine, half):
            for e in range(half * NE // 2, (half + 1) * NE // 2, 8):
                for row in load_many(engine, rowi, e, DUMMY - P):
                    eng.dma_start(xs[bass.ds(row, P), :], zeros).then_inc(s["zero_done"], 16)

        def row_stats(dve, step, src):
            for n in range(NT):
                last = dve.bn_stats(stats[:, n, :], src[:, n, :])
            step(last)

        def tok(buf, b, t=0, n=1):
            return buf[:, bass.ds(b * TPB + t, n), :]

        def tok1(buf, b, t):
            return tok(buf, b, t).rearrange("p a d -> p (a d)")

        @block.sync
        def _(sp):
            for dst, src in ((csb[:, :], c), ):
                sp.dma_start(dst, src).then_inc(s["ld_c"], 16)
            sp.dma_start(modb[:, 0:2, :, :].rearrange("p a b d -> p (a b d)")[:, 0:6 * D], wmod).then_inc(s["ld_c"], 16)
            sp.dma_start(relb[:, :], rel_bias).then_inc(s["ld_b"], 16)
            sp.dma_start(oneh[:, :], onehot).then_inc(s["ld_b"], 16)
            sp.dma_start(scol[:, :], scale.rearrange("(h a) -> h a", a=1)).then_inc(s["ld_b"], 16)
            sp.dma_start(srow[:, :], scale.rearrange("(a h) -> a h", a=1).to_broadcast([P, H])).then_inc(s["ld_b"], 16)
            xv = x.rearrange("b (t p) d -> p (b t) d", p=P)
            for i in range(4):
                sp.dma_start(X[:, i * 8:(i + 1) * 8, :], xv[:, i * 8:(i + 1) * 8, :]).then_inc(s["ld_x"], 16)
            for dst, src in ((wqkv[:, 0:D], Wq), (wqkv[:, D:2 * D], Wk), (wqkv[:, 2 * D:], Wv), (wo[:, :], Wo),
                             (w1s[:, :], W1), (w2s[:, :, :], W2.rearrange("(c p) d -> p c d", p=P)),
                             (ln1[:, :], ln1_w.rearrange("(p a) -> p a", a=1)),
                             (ln2[:, :], ln2_w.rearrange("(p a) -> p a", a=1)), (gate[:, :], gate_w),
                             (ebias[:, :], e_bias.rearrange("(a e) -> a e", a=1).to_broadcast([P, NE])),
                             (w2e[:, :, :], w2.rearrange("e i d -> i e d"))):
                sp.dma_start(dst, src).then_inc(s["ld_w"], 16)
            sp.wait_ge(s["dr_dve"], 2)
            sp.dma_start(dist_row, drow[:, :]).then_inc(s["wr_dist"], 16)
            sp.wait_ge(s["wr_dist"], 16)
            sp.dma_start(dist_rep, dist_row.rearrange("h (a l) -> h a l", a=1).to_broadcast([H, P, RL])).then_inc(s["rep_dist"], 16)
            sp.wait_ge(s["rep_dist"], 16)
            for h in range(H):
                for n, w in ((0, SEQ), (1, P)):
                    src = bass.AP(dist_rep.tensor, h * P * RL + P - 1, [[RL - 1, P], [1, w]])
                    at = (h % 2) * HW + (SEQ if n else 0)
                    sp.dma_start(BIAS[:, h // 2, at:at + w], src).then_inc(s["ld_bias"], 16)
            sp.wait_ge(s["md_dve"], 2)
            sp.dma_start(mod_rows, mrow[:, :, :].rearrange("b m d -> b (m d)")).then_inc(s["wr_mod"], 16)
            sp.wait_ge(s["wr_mod"], 16)
            sp.dma_start(modb[:, :, :, :].rearrange("p b m d -> p (b m d)"),
                         mod_rows.rearrange("b m -> (b m)").rearrange("(a m) -> a m", a=1).to_broadcast([P, NB * 4 * D])
                         ).then_inc(s["ld_mod"], 16)
            sp.wait_ge(s["l_ready"], NB * UNITS + 2)
            w13v = w13.rearrange("p (e g i) -> p e g i", e=NE, g=2)
            sp.dma_start(w13v[:, :, 0, :], w1.rearrange("e d i -> d e i")).then_inc(s["ld_e"], 16)
            sp.dma_start(w13v[:, :, 1, :], w3.rearrange("e d i -> d e i")).then_inc(s["ld_e"], 16)
            sp.wait_ge(s["zero_ready"], 1)
            sp.dma_start(xs[DUMMY:DUMMY + P, :], zeros).then_inc(s["zero_done"], 16)
            sp.wait_ge(s["rows_ready"], 1)
            pad_zeros(sp, mybir.EngineType.SP, 0)
            sp.wait_ge(s["zero_done"], 16 * (NE + 1))
            sp.wait_ge(s["scat0"], 16 * NT * TOPK // 2)
            sp.wait_ge(s["scat1"], 16 * NT * TOPK // 2)
            sp.wait_ge(s["t_ready"], 1)

            rows_of = treg[0:1, 2:4, :].rearrange("p a b -> p (a b)")

            def load_pair(i, buf, transposed=None):
                rows = load_many(mybir.EngineType.SP, rows_of, i * XG, DUMMY)
                if transposed is not None:
                    sp.wait_ge(s["xt_pe"], transposed)
                for j in range(2 * XG):
                    sp.dma_start(xg[buf + j // XG][:, (j % XG) * P:(j % XG + 1) * P],
                                 xs[bass.ds(rows[j], P), :]).then_inc(s[f"x_rows{buf + j // XG}"], 16)
            load_pair(0, 0)
            load_pair(2, 2)
            with sp.Fori(0, XSTEPS // 4 - 1) as four:
                i = four * 4
                for pair in range(2):
                    load_pair(i + 2 * pair + 4, 2 * pair, i + 2 * pair + 2)
            load_pair(XSTEPS, 0, XSTEPS - 4 + 2)
            outv = out.rearrange("b (t p) d -> p (b t) d", p=P)
            with sp.Fori(0, NT // 2) as two:
                n = two * 2
                for par in range(2):
                    sp.wait_ge(s["acc_ready"], n + par + 1)
                    sp.dma_start(outv[:, bass.ds(n + par, 1), :].rearrange("p a d -> p (a d)"),
                                 acc[par][:, :]).then_inc(s[f"ost{par}"], 16)
            for par in range(2):
                sp.wait_ge(s[f"ost{par}"], 16 + 16 * NT // 2)

        @block.gpsimd
        def _(pool):
            st = Steps(pool, "pool_s")
            st(pool.memset(ident[:, :], 0.0))
            st(pool.memset(identb[:, :], 0.0))
            st(pool.memset(tri[:, :], 1.0))
            st.wait()
            for m in (ident, identb):
                pool.affine_select(out=m[:, :], in_=m[:, :], compare_op=ALU.not_equal, fill=1.0, base=0,
                                   pattern=[[-1, P]], channel_multiplier=1)
            pool.affine_select(out=tri[:, :], in_=tri[:, :], compare_op=ALU.is_ge, fill=0.0, base=-1,
                               pattern=[[1, P]], channel_multiplier=-1)
            pool.memset(onesb[:, :], 1.0)
            pool.memset(ones[:, :], 1.0)
            pool.memset(onesf[:, :], 1.0)
            pool.memset(seen[:, :], 0.0)
            pool.iota(iota_e[:, :], [[1, NE]], base=0, channel_multiplier=0, allow_small_or_imprecise_dtypes=True)
            pool.iota(tile_no[:, :], [[P, 2]], base=0, channel_multiplier=1, allow_small_or_imprecise_dtypes=True)
            pool.memset(SLOTS[:, :, :, :], 0.0)
            pool.memset(V[0][:, :, :, :], 0.0)
            st(pool.memset(V[1][:, :, :, :], 0.0))
            st.wait()
            for v in V:
                last = pool.memset(v[:, :, :, HD:HD + 1], 1.0)
            last.then_inc(s["pool_c"], 1)
            pool.wait_ge(s["x_stats"], 1)
            pool.wait_ge(s["gt_dve"], 1)
            pool.wait_ge(s["flag_ready"], 1)
            pool.sem_inc(s["hr_ready"], 2)
            big = pool.value_load(flagi[0:1, 0:1], min_val=0, max_val=1)

            nqk = 2 * TPB * H
            STEPS_N = 15

            def norms(b):
                step = Steps(pool, "pool_n", alone=True)
                step.at = b * STEPS_N
                pool.wait_ge(s["ss_ready"], b + 1)
                settle(pool)
                step(pool.tensor_scalar(em[:, :], arg[:, nqk:], KQ_EPS, None, ALU.mult))
                step.wait()
                step(pool.tensor_tensor(arg[:, 0:nqk].rearrange("p (q t h) -> p q t h", q=2, t=TPB),
                                        nt1[:, 0:nqk].rearrange("p (q t h) -> p q t h", q=2, t=TPB),
                                        em[:, :].unsqueeze(1).unsqueeze(3).to_broadcast([P, 2, TPB, H]), ALU.add))
                step.wait()
                rsqrt(pool, step, rs[:, :], arg[:, :], nt1[:, :], nt2[:, :], fused=False)
                step.wait()
                pool.tensor_tensor(rs[:, 0:TPB * H], rs[:, 0:TPB * H], qscale[:, :, :].rearrange("p t h -> p (t h)"),
                                   ALU.mult).then_inc(s["rs_done"], 1)
                assert step.n == STEPS_N, step.n

            def h_copy(b, par):
                pool.wait_ge(s["o5_done"], b + 1)
                settle(pool)
                pool.wait_ge(s["hT_ready"], b + 1)
                settle(pool)
                pool.tensor_copy(hR[par][:, :], hT[par][:, :]).then_inc(s["hr_ready"], 1)

            def row_max(b, units):
                with pool.If(big == 1):
                    for u in units:
                        pool.wait_ge(s["g_in"], b * UNITS + u + 1)
                        settle(pool)
                        pool.partition_all_reduce(LM[:, :], L[u % 2][:, :], P, RMAX).then_inc(s["g_max"], 1)

            def sequence(b, par, last=False):
                row_max(b, range(0, 2))
                if not last:
                    norms(b + 1)
                row_max(b, range(2, 4))
                if not last:
                    h_copy(b + 1, 1 - par)
                row_max(b, range(4, UNITS))

            norms(0)
            h_copy(0, 0)
            sequence(0, 0)
            with pool.Fori(0, (NB - 2) // 2) as two:
                b = two * 2 + 1
                sequence(b, 1)
                sequence(b + 1, 0)
            sequence(NB - 1, 1, last=True)

            def scatter(g, first=False):
                for j in range(GROUP):
                    b = g * GROUP + j
                    pool.wait_ge(s["pos_ready"], b + 1)
                    settle(pool)
                    for t in range(TPB):
                        for k in range(TOPK):
                            pool.indirect_dma_start(
                                out=xs, out_offset=bass.IndirectOffsetOnAxis(
                                    ap=posi[j][:, t * TOPK + k:t * TOPK + k + 1], axis=0),
                                in_=H2[j][:, t, :], in_offset=None).then_inc(s[f"scat{j % 2}"], 16)
                    if not first or j > 0:
                        pool.wait_ge(s[f"scat{(j + 1) % 2}"], (g * GROUP + j + 1) // 2 * (TPB * TOPK * 16))
                        pool.sem_inc(s["h2_free"], 1)
            pool.sem_inc(s["h2_free"], GROUP)
            scatter(0, first=True)
            with pool.Fori(1, NB // GROUP) as g:
                scatter(g)

            with pool.Fori(0, XSTEPS // 2) as two:
                i = two * 2
                for par in range(2):
                    pool.wait_ge(s["y_ev"], i + par + 1 + 2)
                    settle(pool)
                    pool.dma_start(ys[bass.ds((i + par) * XG * P, XG * P), :].rearrange("(j p) d -> p j d", p=P),
                                   yo[par].rearrange("p (j d) -> p j d", j=XG)).then_inc(s["yst"], 16)
                    pool.wait_ge(s["yst"], 16 * (i + par) + 16)
                    pool.sem_inc(s["y_free"], 1)

            pool.wait_ge(s["pos_all"], 1)
            with pool.Fori(0, NT // 2) as two:
                n = two * 2
                for par in range(2):
                    pool.wait_ge(s["g_free"], n + par + 1)
                    settle(pool)
                    pool.tensor_copy(gidx[par][:, :], POS[:, bass.ds((n + par) * TOPK, TOPK)]).then_inc(s["pool_g"], 1)
                    pool.wait_ge(s["pool_g"], n + par + 1)
                    settle(pool)
                    for k in range(TOPK):
                        pool.indirect_dma_start(out=G[par][:, k, :], out_offset=None, in_=ys,
                                                in_offset=bass.IndirectOffsetOnAxis(ap=gidx[par][:, k:k + 1], axis=0)
                                                ).then_inc(s[f"gsem{par}"], 16)

        @block.scalar
        def _(act):
            act.sem_inc(s["qkt_act"], 2)
            act.sem_inc(s["exp_done"], 2)
            act.sem_inc(s["ynt_ready"], 1)
            act.sem_inc(s["y_ready"], 1)
            act.wait_ge(s["ld_c"], 32)
            act.activation(cth[:, :], csb[:, :], ACT.Tanh, scale=0.5).then_inc(s["sc_act"], 1)

            def make_hT(b, par):
                act.wait_ge(s["xt_done"], b + 1 + 1)
                act.wait_ge(s["hr_ready"], b + 1)
                a, c0 = modT[:, bass.ds(b + NB, 1)], modT[:, bass.ds(b, 1)]
                act.activation(hT[par][:, :], bank(CTX, SEQ, SEQ), ACT.Identity, bias=c0, scale=a)
                act.activation(hsq[:, :], bank(CTX, SEQ, SEQ), ACT.Square, bias=c0, scale=a).then_inc(s["hT_ready"], 1)

            def squares(b):
                act.wait_ge(s["qkv_done"], b + 1)
                act.activation(sq[:, :].rearrange("p (q t d) -> p t q d", q=2, t=TPB),
                               PS[:, PRE:PRE + TPB, 0:2 * D].rearrange("p t (q d) -> p t q d", q=2),
                               ACT.Square).then_inc(s["sq_done"], 1)

            def values(b, par):
                act.wait_ge(s["qn_done"], b + 1)
                for t in range(TPB):
                    last = act.activation(V[par][:, t, :, 0:HD],
                                          bank(PRE + t, D, 2 * D).rearrange("p (h d) -> p h d", h=H),
                                          ACT.Identity, scale=rs[:, 2 * TPB * H + t:2 * TPB * H + t + 1])
                last.then_inc(s["v_ready"], 1)

            def qk_half(b, par, qk):
                act.wait_ge(s["qkt_done"], b * 4 + 2 * qk + 1)
                act.activation(QKT[par][:, qk, :, 0:P], bank(PRE).bitcast(BF16).rearrange("p (u t) -> p u t", u=UNITS),
                               ACT.Copy).then_inc(s["qkt_act"], 1)

            def exp(b, u):
                act.wait_ge(s["l_ready"], b * UNITS + u + 1 + 2)
                if u % 2 == 0:
                    act.wait_ge(s["pv_done"], b * 4 + u // 2 + 1)
                act.activation(PR[u % 4][:, :], L[u % 2][:, :], ACT.Exp).then_inc(s["exp_done"], 1)

            def context(b, half):
                act.wait_ge(s["pv_done"], b * 4 + 2 * half + 2 + 2)
                act.activation(YT[:, 2 * half:2 * half + 2, :].rearrange("p g t -> p (g t)"), bank(CTX + half),
                               ACT.Copy).then_inc(s["yt_ready"], 1)

            def yn_T(b):
                act.wait_ge(s["o4_done"], b + 1)
                act.activation(YNT[:, :], bank(CTX, SEQ), ACT.Copy).then_inc(s["ynt_ready"], 1)

            def y_out(b):
                act.wait_ge(s["o5_done"], b + 1 + 2)
                act.activation(tok(Y, b, 0, TPB), bank(CTX + 1, SEQ).rearrange("p (t d) -> p t d", t=TPB),
                               ACT.Copy).then_inc(s["y_ready"], 1)

            def sequence(b, par, first=False, last=False, last_two=False):
                exp(b, 0)
                exp(b, 1)
                if not last:
                    squares(b + 1)
                if not first:
                    yn_T(b - 1)
                if not last_two:
                    make_hT(b + 2, par)
                exp(b, 2)
                exp(b, 3)
                exp(b, 4)
                exp(b, 5)
                if not first:
                    y_out(b - 1)
                if not last:
                    values(b + 1, 1 - par)
                context(b, 0)
                exp(b, 6)
                exp(b, 7)
                if not last:
                    qk_half(b + 1, 1 - par, 0)
                    qk_half(b + 1, 1 - par, 1)
                context(b, 1)

            act.wait_ge(s["md_dve"], 1)
            make_hT(0, 0)
            squares(0)
            make_hT(1, 1)
            values(0, 0)
            qk_half(0, 0, 0)
            qk_half(0, 0, 1)
            sequence(0, 0, first=True)
            with act.Fori(0, (NB - 4) // 2) as two:
                b = two * 2 + 1
                sequence(b, 1)
                sequence(b + 1, 0)
            sequence(NB - 3, 1)
            sequence(NB - 2, 0, last_two=True)
            sequence(NB - 1, 1, last=True, last_two=True)
            yn_T(NB - 1)
            y_out(NB - 1)

            def group(g, mlp=True, route=True):
                m0, r0 = g * GROUP, (g - 1) * GROUP

                def begin(j):
                    if mlp:
                        act.wait_ge(s["m_t"], m0 + j + 1)
                        act.activation(mT[j % 2], bank(0, SEQ), ACT.Copy).then_inc(s["m_tev"], 1)
                    if route:
                        act.wait_ge(s["r_t"], r0 + j + 1)
                        act.activation(H2T[j % 2], bank(4, SEQ), ACT.Copy).then_inc(s["r_tev"], 1)
                begin(0)
                for j in range(GROUP):
                    if mlp:
                        act.wait_ge(s["m_hid"], m0 + j + 1)
                        act.activation(hid[j % 2][:, 0:2, :].rearrange("p c t -> p (c t)"), bank(1),
                                       ACT.Relu).then_inc(s["relu_act"], 1)
                    if route:
                        act.wait_ge(s["r_lg"], r0 + j + 1)
                        act.activation(th[:, :, :].rearrange("p t e -> p (t e)"), bank(5, TPB * NE),
                                       ACT.Tanh, scale=0.5).then_inc(s["r_th"], 1)
                    if j + 1 < GROUP:
                        begin(j + 1)
            group(0, route=False)
            with act.Fori(1, NB // GROUP) as g:
                group(g)
            group(NB // GROUP, mlp=False)
            def silu(i, par):
                act.wait_ge(s["gu_pe"], i + 1)
                act.wait_ge(s["a_dve"], i + 1)
                act.activation(sg[par].rearrange("p (a b i) -> p a b i", a=2, b=2),
                               PS[:, 2 + 2 * par:4 + 2 * par, 0:4 * INNER]
                               .rearrange("p a (b g i) -> p a b g i", b=2, g=2)[:, :, :, 0, :],
                               ACT.Silu).then_inc(s["sg_act"], 1)

            def a_T(i, par):
                act.wait_ge(s["at_pe"], i + 1)
                act.wait_ge(s["y_pe"], i + 1)
                act.activation(aT[par][0:INNER, :], PS[0:INNER, 2 + 2 * par, :], ACT.Copy).then_inc(s["at_act"], 1)
            act.wait_ge(s["rows_ready"], 1)
            act.wait_ge(s["zero_ready"], 1)
            pad_zeros(act, mybir.EngineType.Activation, 1)
            act.sem_inc(s["at_act"], 2)
            with act.Fori(0, XSTEPS // 2) as two:
                i = two * 2
                for par in range(2):
                    silu(i + par, par)
                for par in range(2):
                    a_T(i + par, par)

        @block.tensor
        def _(pe):
            pe.sem_inc(s["pv_done"], 2)
            pe.sem_inc(s["o5_done"], 2)
            pe.sem_inc(s["xt_done"], 1)
            pe.wait_ge(s["pool_c"], 1)
            pe.wait_ge(s["sc_dve"], 1)
            pe.transpose(bank(0, NB), cth[:, :], ident[0:NB, 0:NB]).then_inc(s["sc_pe"], 1)
            pe.wait_ge(s["sc_dve"], 2)
            wm = modb[:, 0:2, :, :].rearrange("p a b d -> p (a b d)")
            for j in range(2):
                pe.matmul(bank(1, NB, j * NB), wm[:, j * D:(j + 1) * D], scT[:, :], start=True, stop=True)
            pe.matmul(PS[0:NB, 2, :], scT[:, :], wm[:, 2 * D:6 * D], start=True, stop=True).then_inc(s["md_pe"], 1)
            pe.wait_ge(s["ld_b"], 64)
            pe.matmul(PS[0:H, 3, 0:RL], relb[:, :], oneh[:, :], start=True, stop=True).then_inc(s["dr_pe"], 1)
            pe.wait_ge(s["ld_w"], 16 * 11)
            pe.transpose(bank(4, NE), gate[:, :], ident[0:NE, 0:NE]).then_inc(s["gt_pe"], 1)
            pe.wait_ge(s["gt_dve"], 1)

            def x_T(b, first=False):
                pe.wait_ge(s["xh_ready"], b + 1)
                if not first:
                    pe.wait_ge(s["hT_ready"], b)
                for t in range(TPB):
                    last = pe.transpose(bank(CTX, P, SEQ + t * P), XH[:, t, :], ident[:, :])
                last.then_inc(s["xt_done"], 1)

            def qkv(b, par):
                pe.wait_ge(s["hT_ready"], b + 1)
                pe.wait_ge(s["qkt_act"], 2 * b + 2)
                pe.wait_ge(s["qkt_dve"], 2 * b + 2)
                for t in range(TPB):
                    pe.matmul(bank(PRE + t, 3 * D), hT[par][:, t * P:(t + 1) * P], wqkv[:, :], start=True, stop=True)
                    last = pe.matmul(bank(PRE + t, 1, 3 * D), hsq[:, t * P:(t + 1) * P], ones[:, :], start=True, stop=True)
                last.then_inc(s["qkv_done"], 1)

            def qk_T(b, qk):
                pe.wait_ge(s["slots_ready"], b * 2 + qk + 1)
                if qk == 0:
                    pe.wait_ge(s["qn_done"], b + 1)
                    pe.wait_ge(s["v_ready"], b + 1)
                for t in range(TPB):
                    if qk == 1:
                        pe.wait_ge(s["qkt_act" if t == 0 else "qkt_dve"], 2 * b + 1 + 2)
                    for u in range(UNITS):
                        last = pe.transpose(bank(PRE + t).bitcast(BF16)[:, u * P:(u + 1) * P],
                                            SLOTS[:, qk, t * H + 2 * u:t * H + 2 * u + 2, :].rearrange("p h s -> p (h s)"),
                                            identb[:, :])
                    last.then_inc(s["qkt_done"], 1)

            def scores(b, par, u):
                if u == 0:
                    pe.wait_ge(s["qkt_act"], 2 * b + 2 + 2)
                    pe.wait_ge(s["qkt_dve"], 2 * b + 2 + 2)
                pe.wait_ge(s["l_ready"], b * UNITS + u + 1)
                at = S_A if u % 2 == 0 else S_B
                for j in range(2):
                    r = slice(SLOT * j, SLOT * j + 6 * HD)
                    pe.matmul(bank(at + j, SEQ), QKT[par][r, 1, u, 0:P], QKT[par][r, 0, u, :], start=True, stop=True)
                    last = pe.matmul(bank(at + j, P, SEQ), QKT[par][r, 1, u, P:SEQ], QKT[par][r, 0, u, P:SEQ],
                                     start=True, stop=True)
                last.then_inc(s["qk_done"], 1)

            def products(b, par, g, h_done=None):
                pe.wait_ge(s["exp_done"], b * UNITS + 2 * g + 2 + 2)
                if g == 0:
                    pe.wait_ge(s["v_ready"], b + 1)
                    pe.wait_ge(s["ynt_ready"], b + 1)
                    pe.wait_ge(s["hT_ready"], h_done)
                if g == 2:
                    pe.wait_ge(s["y_ready"], b + 1)
                dst = bank(CTX + g // 2, SEQ, (g % 2) * SEQ)
                for j in range(4):
                    h, pr = 4 * g + j, PR[(2 * g + j // 2) % 4]
                    o = dst[32 * j:32 * j + 32, :]
                    pe.matmul(o, V[par][:, 0, h, :], pr[:, (j % 2) * HW:(j % 2) * HW + SEQ],
                              start=True, stop=False, skip_group_check=True)
                    pe.matmul(o[:, P:SEQ], V[par][:, 1, h, :], pr[:, (j % 2) * HW + SEQ:(j % 2 + 1) * HW],
                              start=False, stop=False, skip_group_check=True)
                pe.matmul(dst[:, 0:1], V[par][:, 1, 4 * g:4 * g + 4, :].rearrange("p h d -> p (h d)"), ones[:, :],
                          start=False, stop=True, skip_group_check=True).then_inc(s["pv_done"], 1)

            def ctx_T(b):
                pe.wait_ge(s["yt_ready"], 2 * b + 2)
                for t in range(TPB):
                    for g in range(H // 4):
                        last = pe.transpose(bank(CTX + t, P, g * P), YT[:, g, t * P:(t + 1) * P], ident[:, :])
                last.then_inc(s["o2_done"], 1)

            def yn_T(b):
                pe.wait_ge(s["o3_done"], b + 1)
                for t in range(TPB):
                    last = pe.transpose(bank(CTX, P, t * P), YN[:, t, :], ident[:, :])
                last.then_inc(s["o4_done"], 1)

            def y_out(b, par):
                pe.wait_ge(s["ynt_ready"], b + 1 + 1)
                pe.wait_ge(s["hr_ready"], b + 1 + 2)
                for t in range(TPB):
                    cols = slice(t * P, (t + 1) * P)
                    pe.matmul(bank(CTX + 1, P, t * P), YNT[:, cols], wo[:, :], start=True, stop=False)
                    last = pe.matmul(bank(CTX + 1, P, t * P), hR[par][:, cols], ident[:, :], start=False, stop=True)
                last.then_inc(s["o5_done"], 1)

            def sequence(b, par, first=False, last=False, last_two=False):
                scores(b, par, 0)
                scores(b, par, 1)
                if not last:
                    qkv(b + 1, 1 - par)
                if not first:
                    ctx_T(b - 1)
                scores(b, par, 2)
                scores(b, par, 3)
                if not first:
                    pe.wait_ge(s["o3_done"], b)
                if not last_two:
                    x_T(b + 2)
                if not first:
                    yn_T(b - 1)
                scores(b, par, 4)
                scores(b, par, 5)
                products(b, par, 0, NB if last_two else b + 3)
                if not first:
                    y_out(b - 1, 1 - par)
                scores(b, par, 6)
                products(b, par, 1)
                scores(b, par, 7)
                if not last:
                    qk_T(b + 1, 0)
                products(b, par, 2)
                if not last:
                    qk_T(b + 1, 1)
                products(b, par, 3)

            x_T(0, first=True)
            qkv(0, 0)
            x_T(1)
            qk_T(0, 0)
            qk_T(0, 1)
            sequence(0, 0, first=True)
            with pe.Fori(0, (NB - 4) // 2) as two:
                b = two * 2 + 1
                sequence(b, 1)
                sequence(b + 1, 0)
            sequence(NB - 3, 1)
            sequence(NB - 2, 0, last_two=True)
            sequence(NB - 1, 1, last=True, last_two=True)
            ctx_T(NB - 1)
            yn_T(NB - 1)
            y_out(NB - 1, 1)

            pe.wait_ge(s["y_ready"], NB + 1)

            def group(g, mlp=True, route=True):
                m0, r0 = g * GROUP, (g - 1) * GROUP

                def begin(j):
                    if mlp:
                        pe.wait_ge(s["ys_staged"], m0 + j + 1)
                        for t in range(TPB):
                            last = pe.transpose(bank(0, P, t * P), YS[j % 2][:, t, :], ident[:, :])
                        last.then_inc(s["m_t"], 1)
                    if route:
                        pe.wait_ge(s["h2_ready"], r0 + j + 1)
                        for t in range(TPB):
                            last = pe.transpose(bank(4, P, t * P), H2[j][:, t, :], ident[:, :])
                        last.then_inc(s["r_t"], 1)

                def hidden(j):
                    pe.wait_ge(s["m_tev"], m0 + j + 1)
                    for ch in range(HID // P):
                        last = pe.matmul(bank(1 + ch // 2, SEQ, (ch % 2) * SEQ), w1s[:, ch * P:(ch + 1) * P],
                                         mT[j % 2], start=True, stop=True)
                    last.then_inc(s["m_hid"], 1)

                def logits(j):
                    pe.wait_ge(s["r_tev"], r0 + j + 1)
                    for t in range(TPB):
                        last = pe.matmul(bank(5, NE, t * NE), H2T[j % 2][:, t * P:(t + 1) * P], gateT[:, :],
                                         start=True, stop=True)
                    last.then_inc(s["r_lg"], 1)

                def mlp_out(j):
                    pe.wait_ge(s["relu_act"], m0 + j + 1)
                    pe.wait_ge(s["relu_dve"], m0 + j + 1)
                    pe.wait_ge(s["z_done"], m0 + j + 1)
                    for t in range(TPB):
                        for ch in range(HID // P):
                            last = pe.matmul(bank(3, P, t * P), hid[j % 2][:, ch, t * P:(t + 1) * P], w2s[:, ch, :],
                                             start=(ch == 0), stop=(ch == HID // P - 1))
                    last.then_inc(s["m_z"], 1)

                def ranks(j):
                    pe.wait_ge(s["r_mask"], r0 + j + 1)
                    pe.matmul(bank(6, NE), tri[:, :], maskb[:, 0, :], start=True, stop=False)
                    pe.matmul(bank(6, NE), onesb[:, :], seen[:, :], start=False, stop=True)
                    pe.matmul(bank(6, NE, NE), tri[:, :], maskb[:, 1, :], start=True, stop=False)
                    pe.matmul(bank(6, NE, NE), onesb[:, :], maskb[:, 0, :], start=False, stop=False)
                    pe.matmul(bank(6, NE, NE), onesb[:, :], seen[:, :], start=False, stop=True).then_inc(s["r_rank"], 1)
                begin(0)
                if route:
                    logits(0)
                if mlp:
                    hidden(0)
                for j in range(GROUP):
                    if mlp:
                        mlp_out(j)
                    if j + 1 < GROUP:
                        begin(j + 1)
                        if mlp:
                            hidden(j + 1)
                    if route:
                        ranks(j)
                        if j + 1 < GROUP:
                            logits(j + 1)
            group(0, route=False)
            with pe.Fori(1, NB // GROUP) as g:
                group(g)
            group(NB // GROUP, mlp=False)
            pe.wait_ge(s["pos_ready"], NB)
            pe.matmul(bank(0, NE), onesb[:, :], seen[:, :], start=True, stop=True).then_inc(s["cnt_pe"], 1)
            pe.wait_ge(s["tv_ready"], 1)
            for j in range(4):
                last = pe.matmul(PS[0:1, 1, j * P:(j + 1) * P], tv[:, j:j + 1], ident[:, :], start=True, stop=True)
            last.then_inc(s["tv_pe"], 1)
            pe.wait_ge(s["t_ready"], 1)
            pe.wait_ge(s["ld_e"], 32)
            e_of = treg[0:1, 0:2, :].rearrange("p a b -> p (a b)")
            w2f = w2e[:, :, :].rearrange("i e d -> i (e d)")

            def rows_T(i, buf, turn):
                pe.wait_ge(s[f"x_rows{buf}"], 16 * XG * (turn + 1))
                pe.wait_ge(s["xt_ev"], i + 1)
                for j in range(XG):
                    last = pe.transpose(bank(buf % 2, P, j * P), xg[buf][:, j * P:(j + 1) * P], ident[:, :])
                last.then_inc(s["xt_pe"], 1)

            def gate_up(i, par, experts):
                pe.wait_ge(s["xt_ev"], i + 1 + 2)
                pe.wait_ge(s["a_dve"], i + 1)
                pe.wait_ge(s["at_act"], i + 1)
                settle(pe)
                for j, e in enumerate(experts):
                    last = pe.matmul(bank(2 + 2 * par + j // 2, 2 * INNER, (j % 2) * 2 * INNER),
                                     xgT[par][:, j * P:(j + 1) * P], w13[:, bass.ds(e * (2 * INNER), 2 * INNER)],
                                     start=True, stop=True)
                last.then_inc(s["gu_pe"], 1)

            def a_T(i, par):
                pe.wait_ge(s["a_dve"], i + 1 + 2)
                for j in range(XG):
                    last = pe.transpose(PS[0:INNER, 2 + 2 * par, j * P:(j + 1) * P], aa[par][:, j * INNER:(j + 1) * INNER],
                                        ident[:, :])
                last.then_inc(s["at_pe"], 1)

            def down(i, par, experts):
                pe.wait_ge(s["at_act"], i + 1 + 2)
                pe.wait_ge(s["y_ev"], i + 1)
                settle(pe)
                for j, e in enumerate(experts):
                    last = pe.matmul(bank(6 + par, P, j * P), aT[par][0:INNER, j * P:(j + 1) * P], w2f[:, bass.ds(e * D, D)],
                                     start=True, stop=True)
                last.then_inc(s["y_pe"], 1)

            pe.sem_inc(s["y_pe"], 2)
            rows_T(0, 0, 0)
            rows_T(1, 1, 0)
            with pe.Fori(0, XSTEPS // 8) as eight:
                ex_next = load_many(mybir.EngineType.PE, e_of, eight * (8 * XG), NE - 1)
                for pair in range(4):
                    i = eight * 8 + 2 * pair
                    ex = ex_next
                    gate_up(i, 0, ex[:XG])
                    gate_up(i + 1, 1, ex[XG:])
                    ex_next = []
                    for par in range(2):
                        rows_T(i + 2 + par, (2 * pair + 2) % 4 + par, eight * 2 + (2 * pair + 2) // 4)
                        if pair < 3:
                            ex_next += load_many(mybir.EngineType.PE, e_of, (i + 2 + par) * XG, NE - 1, XG)
                        a_T(i + par, par)
                    for par in range(2):
                        down(i + par, par, ex[par * XG:(par + 1) * XG])

        @block.vector
        def _(dve):
            st = Steps(dve, "dve_s")
            dve.sem_inc(s["qkt_dve"], 2)
            dve.sem_inc(s["l_ready"], 2)
            dve.sem_inc(s["z_done"], 1)
            dve.sem_inc(s["xt_ev"], 2)
            dve.sem_inc(s["a_dve"], 2)
            dve.sem_inc(s["y_ev"], 2)
            dve.sem_inc(s["y_free"], 2)
            dve.sem_inc(s["g_free"], 2)
            for n in range(2):
                dve.sem_inc(s[f"ost{n}"], 16)
            dve.wait_ge(s["sc_act"], 1)
            st(dve.tensor_scalar(cth[:, :], cth[:, :], 0.5, 0.5, ALU.mult, ALU.add))
            st.wait()
            dve.tensor_tensor(cth[:, :], cth[:, :], csb[:, :], ALU.mult).then_inc(s["sc_dve"], 1)
            dve.wait_ge(s["sc_pe"], 1)
            dve.tensor_copy(scT[:, :], bank(0, NB)).then_inc(s["sc_dve"], 1)
            dve.wait_ge(s["md_pe"], 1)
            dve.tensor_copy(modT[:, 0:NB], bank(1, NB))
            dve.tensor_scalar(modT[:, NB:], bank(1, NB, NB), 1.0, None, ALU.add).then_inc(s["md_dve"], 1)
            st(dve.tensor_copy(mrow[:, :, :].rearrange("b m d -> b (m d)"), PS[0:NB, 2, :]))
            st.wait()
            gg = mrow[:, 0:4:3, :]
            st(dve.scalar_tensor_tensor(mtmp[:, :, :], gg, -1.0, gg, ALU.mult, ALU.max))
            st.wait()
            st(dve.tensor_scalar(mtmp[:, :, :], mtmp[:, :, :], 0.25, None, ALU.max))
            st(dve.tensor_scalar(gg, gg, 0.0, 2.0, ALU.is_ge, ALU.mult))
            st(dve.tensor_scalar(mrow[:, 2, :], mrow[:, 2, :], 1.0, None, ALU.add))
            st.wait()
            dve.scalar_tensor_tensor(gg, gg, -1.0, mtmp[:, :, :], ALU.add, ALU.mult).then_inc(s["md_dve"], 1)
            dve.wait_ge(s["dr_pe"], 1)
            dve.wait_ge(s["ld_b"], 64)
            dve.tensor_scalar(drow[:, :], PS[0:H, 3, 0:RL], scol[:, 0:1], None, ALU.mult).then_inc(s["dr_dve"], 1)
            dve.wait_ge(s["dr_dve"], 1)
            st(dve.tensor_reduce(flagf[0:H, 0:1], drow[:, :], AX_X, ALU.max, apply_absolute_value=True))
            st(dve.scalar_tensor_tensor(flagf[0:H, 1:2], scol[:, :], -1.0, scol[:, :], ALU.mult, ALU.max))
            st.wait()
            st(dve.tensor_tensor(flagf[0:H, 2:3], flagf[0:H, 0:1], flagf[0:H, 1:2], ALU.add))
            dve.memset(drow[:, 0:P], MASKED).then_inc(s["dr_dve"], 1)
            dve.wait_ge(s["ld_w"], 16 * 11)
            dve.wait_ge(s["gt_pe"], 1)
            dve.tensor_scalar(wqkv[:, :], wqkv[:, :], ln1[:, 0:1], None, ALU.mult)
            dve.tensor_scalar(w1s[:, :], w1s[:, :], ln2[:, 0:1], None, ALU.mult)
            st(dve.tensor_copy(qscale[:, :, :], srow[:, :].unsqueeze(1).to_broadcast([P, TPB, H])))
            st.wait()
            dve.memset(qscale[0:1, 0, :], 0.0)
            dve.tensor_copy(gateT[:, :], bank(4, NE)).then_inc(s["gt_dve"], 1)
            dve.wait_ge(s["pool_c"], 1)
            st(dve.memset(nt1[0:32, 0:32], 0.0))
            st.wait()
            st(dve.tensor_copy(nt1[0:H, 0:1], flagf[0:H, 2:3]))
            st.wait()
            st(dve.transpose(nt2[0:32, 0:32], nt1[0:32, 0:32]))
            st.wait()
            st(dve.tensor_reduce(flagf[0:1, 3:4], nt2[0:1, 0:32], AX_X, ALU.max))
            st.wait()
            st(dve.tensor_scalar(flagf[0:1, 3:4], flagf[0:1, 3:4], SAFE, -1.0, ALU.is_le, ALU.mult))
            st.wait()
            dve.tensor_scalar(flagi[0:1, 0:1], flagf[0:1, 3:4], 1.0, None, ALU.add).then_inc(s["flag_ready"], 1)
            dve.wait_ge(s["ld_x"], 64)
            row_stats(dve, st, X)
            mean_var(dve, st)
            st.wait()
            st(dve.tensor_scalar(var[:, :], var[:, :], LN_EPS, None, ALU.add))
            st.wait()
            rsqrt(dve, st, rstd[:, :], var[:, :], st1[:, :], st2[:, :])
            st.wait()
            dve.sem_inc(s["x_stats"], 1)
            dve.wait_ge(s["flag_ready"], 1)
            big = dve.value_load(flagi[0:1, 0:1], min_val=0, max_val=1)
            nqk = 2 * TPB * H

            def x_hat(b):
                dve.wait_ge(s["xt_done"], b + 1)
                for t in range(TPB):
                    last = dve.tensor_scalar(XH[:, t, :], tok1(X, b, t), mean[:, bass.ds(b * TPB + t, 1)],
                                              rstd[:, bass.ds(b * TPB + t, 1)], ALU.subtract, ALU.mult)
                last.then_inc(s["xh_ready"], 1)

            def sums(b):
                dve.wait_ge(s["sq_done"], b + 1)
                dve.tensor_reduce(nt1[:, 0:nqk], sq[:, :].rearrange("p (n d) -> p n d", d=HD), AX_X, ALU.add)
                dve.tensor_scalar(arg[:, nqk:], PS[:, PRE:PRE + TPB, 3 * D], 1.0 / D, RMS_EPS, ALU.mult, ALU.add
                                  ).then_inc(s["ss_ready"], 1)

            def normalize_qk(b):
                dve.wait_ge(s["rs_done"], b + 1)
                for t in range(TPB):
                    last = dve.tensor_tensor(
                        QKN[:, :].rearrange("p (q t h d) -> p q t h d", q=2, t=TPB, h=H)[:, :, t, :, :],
                        bank(PRE + t, 2 * D).rearrange("p (q h d) -> p q h d", q=2, h=H),
                        rs[:, 0:nqk].rearrange("p (q t h) -> p q t h", q=2, t=TPB)[:, :, t, :].unsqueeze(3)
                        .to_broadcast([P, 2, H, HD]), ALU.mult)
                last.then_inc(s["qn_done"], 1)

            def slot(qk, at, n=1, every=1):
                v = SLOTS[:, qk, :, :].rearrange("p th (n e) -> p th n e", e=HD)
                return v[:, :, at:at + every * (n - 1) + 1:every, :]

            def split(b):
                dve.wait_ge(s["qn_done"], b + 1)
                qn, qr = ([v[:, qk * SEQ:(qk + 1) * SEQ].rearrange("p (th d) -> p th d", d=HD) for qk in range(2)]
                          for v in (QKN, QKR))

                def copies(v, n):
                    return v.unsqueeze(2).to_broadcast([P, TPB * H, n, HD])
                dve.tensor_copy(slot(0, 0, 3), copies(qn[0], 3)).then_inc(s["parts"], 1)
                dve.tensor_copy(slot(1, 1, 3, 2), copies(qn[1], 3)).then_inc(s["parts"], 1)
                dve.wait_ge(s["parts"], b * 6 + 1)
                dve.tensor_tensor(qr[0], qn[0], slot(0, 0)[:, :, 0, :], ALU.subtract).then_inc(s["parts"], 1)
                dve.wait_ge(s["parts"], b * 6 + 2)
                dve.tensor_tensor(qr[1], qn[1], slot(1, 1)[:, :, 0, :], ALU.subtract).then_inc(s["parts"], 1)
                dve.wait_ge(s["parts"], b * 6 + 3)
                dve.tensor_copy(slot(0, 3, 2), copies(qr[0], 2)).then_inc(s["parts"], 1)
                dve.wait_ge(s["parts"], b * 6 + 4)
                dve.tensor_copy(slot(1, 2, 2, 2), copies(qr[1], 2)).then_inc(s["parts"], 1)
                dve.wait_ge(s["parts"], b * 6 + 5)
                dve.tensor_tensor(slot(0, 5)[:, :, 0, :], qr[0], slot(0, 3)[:, :, 0, :], ALU.subtract
                                  ).then_inc(s["slots_ready"], 1)
                dve.wait_ge(s["parts"], b * 6 + 6)
                dve.tensor_tensor(slot(1, 0)[:, :, 0, :], qr[1], slot(1, 2)[:, :, 0, :], ALU.subtract
                                  ).then_inc(s["slots_ready"], 1)

            def qk_half(b, par, qk):
                dve.wait_ge(s["qkt_done"], b * 4 + 2 * qk + 2)
                dve.tensor_copy(QKT[par][:, qk, :, P:SEQ], bank(PRE + 1).bitcast(BF16).rearrange("p (u t) -> p u t", u=UNITS)
                                ).then_inc(s["qkt_dve"], 1)

            def add(b, u):
                dve.wait_ge(s["qk_done"], b * UNITS + u + 1)
                dve.wait_ge(s["exp_done"], b * UNITS + u + 1)
                settle(dve)
                at = S_A if u % 2 == 0 else S_B

                def plus_bias():
                    return dve.tensor_tensor(L[u % 2][:, :].rearrange("p (j w) -> p j w", j=2), PS[:, at:at + 2, 0:HW],
                                             BIAS[:, u, :].rearrange("p (j w) -> p j w", j=2), ALU.add)
                with dve.If(big == 1):
                    plus_bias().then_inc(s["g_in"], 1)
                    dve.wait_ge(s["g_max"], b * UNITS + u + 1)
                    m = LM[:, :].rearrange("p (j w) -> p j w", j=2)
                    v = L[u % 2][:, :].rearrange("p (j w) -> p j w", j=2)
                    dve.tensor_tensor(m[:, :, P:SEQ], m[:, :, P:SEQ], m[:, :, SEQ:], ALU.max).then_inc(s["g_dve"], 1)
                    dve.wait_ge(s["g_dve"], b * UNITS + u + 1)
                    dve.tensor_tensor(v[:, :, 0:SEQ], v[:, :, 0:SEQ], m[:, :, 0:SEQ], ALU.subtract)
                    dve.tensor_tensor(v[:, :, SEQ:], v[:, :, SEQ:], m[:, :, P:SEQ], ALU.subtract).then_inc(s["l_ready"], 1)
                with dve.Else():
                    plus_bias().then_inc(s["l_ready"], 1)

            def normalize(b):
                dve.wait_ge(s["o2_done"], b + 1)
                v = PS[:, CTX:CTX + TPB, :].rearrange("p t (h s) -> p t h s", s=32)
                dve.reciprocal(rden[:, :, :], v[:, :, :, HD]).then_inc(s["c_s"], 1)
                dve.wait_ge(s["c_s"], b + 1)
                dve.tensor_tensor(YN[:, :, :].rearrange("p t (h d) -> p t h d", d=HD), v[:, :, :, 0:HD],
                                  rden[:, :, :].unsqueeze(3).to_broadcast([P, TPB, H, HD]), ALU.mult).then_inc(s["o3_done"], 1)

            def sequence(b, par, first=False, last=False, last_two=False):
                add(b, 0)
                add(b, 1)
                if not last_two:
                    x_hat(b + 2)
                if not last:
                    sums(b + 1)
                if not first:
                    normalize(b - 1)
                for u in range(2, 6):
                    add(b, u)
                if not last:
                    normalize_qk(b + 1)
                    split(b + 1)
                add(b, 6)
                add(b, 7)
                if not last:
                    qk_half(b + 1, 1 - par, 0)
                    qk_half(b + 1, 1 - par, 1)

            x_hat(0)
            x_hat(1)
            sums(0)
            normalize_qk(0)
            split(0)
            qk_half(0, 0, 0)
            qk_half(0, 0, 1)
            dve.wait_ge(s["ld_bias"], 16 * 2 * H)
            dve.memset(BIAS[:, :, 0:HW + 1:HW], 0.0).then_inc(s["bias0"], 1)
            dve.wait_ge(s["bias0"], 1)
            sequence(0, 0, first=True)
            with dve.Fori(0, (NB - 4) // 2) as two:
                b = two * 2 + 1
                sequence(b, 1)
                sequence(b + 1, 0)
            sequence(NB - 3, 1)
            sequence(NB - 2, 0, last_two=True)
            sequence(NB - 1, 1, last=True, last_two=True)
            normalize(NB - 1)

            dve.wait_ge(s["y_ready"], NB + 1)
            row_stats(dve, st, Y)
            mean_var(dve, st)
            st.wait()
            st(dve.tensor_tensor(st1[:, :], mean[:, :], mean[:, :], ALU.mult))
            st.wait()
            st(dve.scalar_tensor_tensor(var[:, :], st1[:, :], RMS_EPS, var[:, :], ALU.add, ALU.add))
            st.wait()
            rsqrt(dve, st, rstd[:, :], var[:, :], st1[:, :], st2[:, :])
            st.wait()
            dve.wait_ge(s["ld_mod"], 16)
            dve.memset(zeros, 0.0).then_inc(s["zero_ready"], 1)
            STEPS_M, STEPS_R, STEPS_G = 4, 13, 17

            def stage(b, par):
                dve.tensor_scalar(YS[par], tok(Y, b, 0, TPB), 0.0, None, ALU.add).then_inc(s["ys_staged"], 1)

            def relu(b, par):
                dve.wait_ge(s["m_hid"], b + 1)
                dve.tensor_scalar(hid[par][:, 2:4, :].rearrange("p c t -> p (c t)"), bank(2), 0.0, None,
                                  ALU.max).then_inc(s["relu_dve"], 1)

            def mlp_out(b, j):
                step = Steps(dve, "m_s")
                step.at = b * STEPS_M
                dve.wait_ge(s["m_z"], b + 1)
                for t in range(TPB):
                    last = dve.scalar_tensor_tensor(zt[:, t, :], bank(3, P, t * P), rstd[:, bass.ds(b * TPB + t, 1)],
                                                    YS[j % 2][:, t, :], ALU.mult, ALU.add)
                last.then_inc(s["z_done"], 1)
                dve.wait_ge(s["z_done"], b + 1 + 1)
                step(dve.tensor_tensor(zt[:, :, :], zt[:, :, :], modb[:, bass.ds(b, 1), 0, :].to_broadcast([P, TPB, D]),
                                       ALU.mult))
                step.wait()
                step(dve.tensor_tensor(tok(X, b, 0, TPB), tok(X, b, 0, TPB), zt[:, :, :], ALU.add))
                step.wait()
                settle(dve)
                for t in range(TPB):
                    step(dve.bn_stats(stats[:, j * TPB + t, :], tok1(X, b, t)))
                step.wait()
                assert step.n == STEPS_M, step.n

            def group_stats(g):
                step = Steps(dve, "rg_s")
                step.at = g * STEPS_G
                mean_var(dve, step, GROUP * TPB, mean_g, var_g, tg[0], tg[1], tg[2])
                step.wait()
                step(dve.tensor_scalar(var_g[:, :], var_g[:, :], LN_EPS, None, ALU.add))
                step.wait()
                rsqrt(dve, step, rstd_g[:, :], var_g[:, :], tg[1][:, :], tg[2][:, :])
                step.wait()
                assert step.n == STEPS_G, step.n

            def modulated(b, j):
                step = Steps(dve, "h_s")
                step.at = b * 2
                dve.wait_ge(s["h2_free"], b + 1)
                for t in range(TPB):
                    c_ = j * TPB + t
                    last = dve.tensor_scalar(H2[j][:, t, :], tok1(X, b, t), mean_g[:, c_:c_ + 1], rstd_g[:, c_:c_ + 1],
                                             ALU.subtract, ALU.mult)
                step(last)
                step.wait()
                step(dve.tensor_tensor(H2[j], H2[j], modb[:, bass.ds(b, 1), 2, :].to_broadcast([P, TPB, D]), ALU.mult))
                step.wait()
                dve.tensor_tensor(H2[j], H2[j], modb[:, bass.ds(b, 1), 1, :].to_broadcast([P, TPB, D]),
                                  ALU.add).then_inc(s["h2_ready"], 1)

            ids = nt1[:, 0:TPB * TOPK]
            oht = OHT[:, :, :, :].rearrange("p t k e -> p (t k) e")

            def pick(b):
                step = Steps(dve, "rt_s")
                step.at = b * STEPS_R
                dve.wait_ge(s["r_th"], b + 1)
                step(dve.tensor_scalar(score[:, :, :], th[:, :, :], 0.5, 0.5, ALU.mult, ALU.add))
                step.wait()
                step(dve.tensor_tensor(sel[:, :, :], score[:, :, :], ebias[:, :].unsqueeze(1).to_broadcast([P, TPB, NE]), ALU.add))
                step.wait()
                settle(dve)
                for t in range(TPB):
                    last = dve.max(top[:, t, :], sel[:, t, :])
                step(last)
                step.wait()
                settle(dve)
                for t in range(TPB):
                    last = dve.max_index(topi[:, t, :], top[:, t, :], sel[:, t, :])
                step(last)
                step.wait()
                step(dve.tensor_copy(ids.rearrange("p (t k) -> p t k", t=TPB), topi[:, :, 0:TOPK]))
                step.wait()
                oh = OH[:, :, :, :].rearrange("p t k e -> p (t k) e")
                step(dve.tensor_tensor(oh, iota_e[:, :].unsqueeze(1).to_broadcast([P, TPB * TOPK, NE]),
                                       ids.unsqueeze(2).to_broadcast([P, TPB * TOPK, NE]), ALU.is_equal))
                step.wait()
                dve.tensor_reduce(maskb[:, :, :], OH[:, :, :, :].rearrange("p t k e -> p t e k"), AX_X, ALU.max
                                  ).then_inc(s["r_mask"], 1)
                dve.tensor_scalar(IDX[:, bass.ds(b * TPB * TOPK, TPB * TOPK)], ids, 0.0, None, ALU.add)
                step(dve.tensor_tensor(OHT[:, :, :, :], OH[:, :, :, :],
                                       score[:, :, :].unsqueeze(2).to_broadcast([P, TPB, TOPK, NE]), ALU.mult))
                step.wait()
                step(dve.tensor_reduce(rk[:, :], oht, AX_X, ALU.add))
                step.wait()
                step(dve.tensor_reduce(wsum[:, :], rk[:, :].rearrange("p (t k) -> p t k", t=TPB), AX_X, ALU.add))
                step.wait()
                step(dve.reciprocal(wsum[:, :], wsum[:, :]))
                step.wait()
                dve.tensor_tensor(WT[:, bass.ds(b * TPB * TOPK, TPB * TOPK)].rearrange("p (t k) -> p t k", t=TPB),
                                  rk[:, :].rearrange("p (t k) -> p t k", t=TPB),
                                  wsum[:, :].unsqueeze(2).to_broadcast([P, TPB, TOPK]), ALU.mult)
                assert step.n == STEPS_R - 3, step.n

            def place(b, j):
                step = Steps(dve, "rt_s", start=STEPS_R - 3)
                step.at = b * STEPS_R
                dve.wait_ge(s["r_rank"], b + 1)
                step(dve.tensor_tensor(OHT[:, :, :, :], OH[:, :, :, :],
                                       bank(6, TPB * NE).rearrange("p (t e) -> p t e", t=TPB).unsqueeze(2)
                                       .to_broadcast([P, TPB, TOPK, NE]), ALU.mult))
                step(dve.tensor_tensor(seen[:, :], seen[:, :], maskb[:, 0, :], ALU.add))
                step.wait()
                dve.tensor_tensor(seen[:, :], seen[:, :], maskb[:, 1, :], ALU.add)
                step(dve.tensor_reduce(rk[:, :], oht, AX_X, ALU.add))
                step.wait()
                dve.tensor_scalar(RK[:, bass.ds(b * TPB * TOPK, TPB * TOPK)], rk[:, :], 0.0, None, ALU.add)
                dve.scalar_tensor_tensor(posi[j][:, :], ids, float(REGION), rk[:, :], ALU.mult, ALU.add
                                         ).then_inc(s["pos_ready"], 1)
                assert step.n == STEPS_R, step.n

            def group(g, mlp=True, route=True):
                m0, r0 = g * GROUP, (g - 1) * GROUP

                def begin(j):
                    if mlp:
                        stage(m0 + j, j % 2)
                    if route:
                        modulated(r0 + j, j)
                begin(0)
                for j in range(GROUP):
                    m, r = m0 + j, r0 + j
                    if mlp:
                        relu(m, j % 2)
                    if j + 1 < GROUP:
                        begin(j + 1)
                    if route:
                        pick(r)
                    if mlp:
                        mlp_out(m, j)
                    if route:
                        place(r, j)
                if mlp:
                    group_stats(g)
            group(0, route=False)
            with dve.Fori(1, NB // GROUP) as g:
                group(g)
            group(NB // GROUP, mlp=False)

            dve.wait_ge(s["cnt_pe"], 1)
            st(dve.tensor_copy(cnt[:, :], bank(0, NE)))
            st.wait()
            dve.scalar_tensor_tensor(rowi[:, :], iota_e[0:1, :], float(REGION), cnt[0:1, :], ALU.mult, ALU.add
                                     ).then_inc(s["rows_ready"], 1)
            st(dve.tensor_scalar(cnti[:, :], cnt[:, :], float(P - 1), None, ALU.add))
            st.wait()
            st(dve.tensor_scalar(cnti[:, :], cnti[:, :], 7, None, ALU.logical_shift_right))
            st.wait()
            st(dve.tensor_copy(ntile[:, :], cnti[:, :]))
            st.wait()
            st(dve.tensor_tensor_scan(tend[:, :], onesf[:, :], ntile[:, :], 0.0, ALU.mult, ALU.add))
            st.wait()
            st(dve.tensor_tensor(tstart[:, :], tend[:, :], ntile[:, :], ALU.subtract))
            for j in range(2):
                last = dve.tensor_scalar(ge[:, j, :], tend[:, :], tile_no[:, j:j + 1], None, ALU.is_le)
            st(last)
            st.wait()
            st(dve.tensor_tensor(ge2[:, :, :], ge[:, :, :], ntile[:, :].unsqueeze(1).to_broadcast([P, 2, NE]), ALU.mult))
            st(dve.tensor_reduce(tv[:, 0:2], ge[:, :, :], AX_X, ALU.add))
            st.wait()
            st(dve.tensor_reduce(tv[:, 2:4], ge2[:, :, :], AX_X, ALU.add))
            st(dve.tensor_scalar(nt1[:, 0:2], tv[:, 0:2], NE - 0.5, float(P), ALU.is_lt, ALU.mult))
            st.wait()
            st(dve.tensor_tensor(nt2[:, 0:2], tile_no[:, :], tv[:, 2:4], ALU.subtract))
            st.wait()
            st(dve.tensor_tensor(nt2[:, 0:2], nt2[:, 0:2], nt1[:, 0:2], ALU.mult))
            st.wait()
            st(dve.scalar_tensor_tensor(tv[:, 2:4], tv[:, 0:2], float(REGION), nt2[:, 0:2], ALU.mult, ALU.add))
            st.wait()
            dve.tensor_scalar(tv[:, 0:2], tv[:, 0:2], float(NE - 1), None, ALU.min).then_inc(s["tv_ready"], 1)
            dve.wait_ge(s["tv_pe"], 1)
            dve.tensor_copy(treg[:, :, :].rearrange("p a b -> p (a b)"), PS[0:1, 1, :]).then_inc(s["t_ready"], 1)
            NPK = NT * TOPK // 4
            big3 = BIG[:, :].rearrange("p (n e) -> p n e", e=NE)
            for q in range(4):
                cs = slice(q * NPK, (q + 1) * NPK)
                st(dve.tensor_tensor(big3, iota_e[:, :].unsqueeze(1).to_broadcast([P, NPK, NE]),
                                     IDX[:, cs].unsqueeze(2).to_broadcast([P, NPK, NE]), ALU.is_equal))
                st.wait()
                st(dve.tensor_tensor(big3, big3, tstart[:, :].unsqueeze(1).to_broadcast([P, NPK, NE]), ALU.mult))
                st.wait()
                st(dve.tensor_reduce(IDX[:, cs], big3, AX_X, ALU.add))
                st.wait()
                last = dve.scalar_tensor_tensor(POS[:, cs], IDX[:, cs], float(P), RK[:, cs], ALU.mult, ALU.add)
            last.then_inc(s["pos_all"], 1)

            def rows_ev(i, par):
                dve.wait_ge(s["xt_pe"], i + 1)
                dve.tensor_copy(xgT[par], bank(par)).then_inc(s["xt_ev"], 1)

            def act_mul(i, par):
                dve.wait_ge(s["sg_act"], i + 1)
                dve.tensor_tensor(aa[par].rearrange("p (a b i) -> p a b i", a=2, b=2),
                                  sg[par].rearrange("p (a b i) -> p a b i", a=2, b=2),
                                  PS[:, 2 + 2 * par:4 + 2 * par, 0:4 * INNER]
                                  .rearrange("p a (b g i) -> p a b g i", b=2, g=2)[:, :, :, 1, :],
                                  ALU.mult).then_inc(s["a_dve"], 1)

            def y_evac(i, par):
                dve.wait_ge(s["y_pe"], i + 1 + 2)
                dve.wait_ge(s["y_free"], i + 1)
                dve.tensor_copy(yo[par], bank(6 + par)).then_inc(s["y_ev"], 1)

            for par in range(2):
                rows_ev(par, par)
            with dve.Fori(0, XSTEPS // 2) as two:
                i = two * 2
                for par in range(2):
                    act_mul(i + par, par)
                    rows_ev(i + 2 + par, par)
                for par in range(2):
                    y_evac(i + par, par)

            with dve.Fori(0, NT // 2) as two:
                n2 = two * 2
                for par in range(2):
                    n = n2 + par
                    dve.wait_ge(s[f"gsem{par}"], n2 * (TOPK * 8) + 16 * TOPK)
                    dve.wait_ge(s[f"ost{par}"], n2 * 8 + 16)
                    dve.tensor_scalar(acc[par][:, :], G[par][:, 0, :], WT[:, bass.ds(n * TOPK, 1)], None, ALU.mult
                                      ).then_inc(s["acc_s"], 1)
                    for k in range(1, TOPK):
                        dve.wait_ge(s["acc_s"], n * 5 + k)
                        dve.scalar_tensor_tensor(acc[par][:, :], G[par][:, k, :], WT[:, bass.ds(n * TOPK + k, 1)],
                                                 acc[par][:, :], ALU.mult, ALU.add).then_inc(s["acc_s"], 1)
                    dve.wait_ge(s["acc_s"], n * 5 + 4)
                    dve.sem_inc(s["g_free"], 1)
                    dve.tensor_tensor(acc[par][:, :], acc[par][:, :],
                                      modb[:, bass.ds(n // TPB, 1), 3, :].rearrange("p a d -> p (a d)"), ALU.mult
                                      ).then_inc(s["acc_s"], 1)
                    dve.wait_ge(s["acc_s"], n * 5 + 5)
                    dve.tensor_tensor(acc[par][:, :], acc[par][:, :],
                                      X[:, bass.ds(n, 1), :].rearrange("p a d -> p (a d)"), ALU.add
                                      ).then_inc(s["acc_ready"], 1)


NAMES = ["x", "ln1_w", "Wq", "Wk", "Wv", "rel_bias", "scale", "Wo", "ln2_w", "W1", "W2", "gate_w", "w1", "w3", "w2",
         "e_bias", "c", "wmod"]


def kernel(L0_attn_x, L0_attn_ln1_w, L0_attn_Wq, L0_attn_Wk, L0_attn_Wv, L0_attn_rel_bias, L0_attn_scale,
           L0_attn_Wo, L0_attn_ln2_w, L0_attn_W1, L0_attn_W2, L0_ffn_gate_w, L0_ffn_w1, L0_ffn_w3, L0_ffn_w2,
           L0_ffn_e_bias, L0_c, L0_wmod):
    import concourse.bacc as bacc
    from concourse.bass_utils import run_bass_kernel_spmd

    values = [L0_attn_x, L0_attn_ln1_w, L0_attn_Wq, L0_attn_Wk, L0_attn_Wv, L0_attn_rel_bias, L0_attn_scale,
              L0_attn_Wo, L0_attn_ln2_w, L0_attn_W1, L0_attn_W2, L0_ffn_gate_w, L0_ffn_w1, L0_ffn_w3, L0_ffn_w2,
              L0_ffn_e_bias, L0_c, L0_wmod, bucket_one_hot()]
    nc = bacc.Bacc("TRN2", target_bir_lowering=False, num_devices=1)
    arrays, args = {}, []
    for name, value in zip(NAMES + ["onehot"], values):
        a = np.ascontiguousarray(value)
        arrays[f"in_{name}"] = a
        args.append(nc.dram_tensor(f"in_{name}", a.shape, mybir.dt.from_np(a.dtype), kind="ExternalInput").ap())
    out = nc.dram_tensor("out", (NB, SEQ, D), F32, kind="ExternalOutput").ap()
    build(nc, *args, out)
    r = run_bass_kernel_spmd(nc, [arrays], core_ids=[0])
    return r.results[0]["out"]
```
